# Optimizing a Trainium2 kernel written in Bass

```python
import numpy as np
import jax
import jax.numpy as jnp

def _softmax(x, axis=-1):
    return jax.nn.softmax(x, axis=axis)

def _gelu(x):
    return jax.nn.gelu(x, approximate=True)

def _silu(x):
    return jax.nn.silu(x)

def _sigmoid(x):
    return jax.nn.sigmoid(x)

def _layernorm(x, axis=-1, eps=1e-05):
    m = jnp.mean(x, axis=axis, keepdims=True)
    v = jnp.var(x, axis=axis, keepdims=True)
    return (x - m) / jnp.sqrt(v + eps)

def _scatter_add(tgt, idx, src, axis=0):
    return tgt.at[idx].add(src)

def _segment_sum(src, seg, n):
    return jax.ops.segment_sum(src, seg, n)
kernel_name = 'mk_gnn_resnorm_d2_gnn_r32_0dcd15'

def setup_inputs(seed: int=0):
    np.random.seed(seed)
    _w = jnp.asarray

    def _rec_inputs():
        import jax
        import jax.numpy as jnp
        _gk = jax.random.key(seed)
        x = -0.000202 + 1 * jax.random.normal(jax.random.fold_in(_gk, 1), (50000, 128), jnp.float32)
        src = jax.random.randint(jax.random.fold_in(_gk, 2), (50000,), 0, 50000, jnp.int32)
        dst = jax.random.randint(jax.random.fold_in(_gk, 3), (50000,), 0, 50000, jnp.int32)
        _o = jnp.argsort(dst, stable=True)
        src = src[_o]
        dst = dst[_o]
        return (x, src, dst)
    x, src, dst = _rec_inputs()

    def _L0_gnn_setup():
        import jax, jax.numpy as jnp
        import numpy as np
        N_NODES = 50000
        N_EDGES = 25000
        IN_DIM = 128
        OUT_DIM = 128
        NUM_HEADS = 8
        HEAD_DIM = OUT_DIM // NUM_HEADS
        LN_EPS = 1e-05
        key = jax.random.key(seed)
        ks = jax.random.split(key, 8)

        def xavier(k, shape, fan_in, fan_out):
            a = float(np.sqrt(6.0 / (fan_in + fan_out)))
            return jax.random.uniform(k, shape, jnp.float32, -a, a)
        x = jax.random.normal(ks[0], (N_NODES, IN_DIM), jnp.float32)
        edge_index = jax.random.randint(ks[1], (2, N_EDGES), 0, N_NODES, jnp.int32)
        W_src = xavier(ks[2], (IN_DIM, OUT_DIM), IN_DIM, OUT_DIM)
        W_dst = xavier(ks[3], (IN_DIM, OUT_DIM), IN_DIM, OUT_DIM)
        attn = xavier(ks[4], (NUM_HEADS, HEAD_DIM), HEAD_DIM, NUM_HEADS)
        W_out = xavier(ks[5], (OUT_DIM, OUT_DIM), OUT_DIM, OUT_DIM)
        b_out = jnp.zeros((OUT_DIM,), jnp.float32)
        gamma = jnp.ones((OUT_DIM,), jnp.float32)
        beta = jnp.zeros((OUT_DIM,), jnp.float32)
        return {'x': x, 'edge_index': edge_index, 'W_src': W_src, 'W_dst': W_dst, 'attn': attn, 'W_out': W_out, 'b_out': b_out, 'gamma': gamma, 'beta': beta}
    _L0_gnn_all = _L0_gnn_setup()
    _L0_gnn_in = {k: v for k, v in _L0_gnn_all.items() if k in ('W_src', 'W_dst', 'attn', 'W_out', 'b_out', 'gamma', 'beta')}
    del _L0_gnn_all

    def _L1_gnn_setup():
        import jax, jax.numpy as jnp
        import numpy as np
        N_NODES = 1250
        N_EDGES = 20000
        D = 128
        L = 3

        def _linear_init(key, fan_in, shape):
            s = 1.0 / np.sqrt(fan_in)
            return jax.random.uniform(key, shape, minval=-s, maxval=s, dtype=jnp.float32)
        key = jax.random.key(seed)
        ks = jax.random.split(key, 10)
        x = jax.random.normal(ks[0], (N_NODES, D), dtype=jnp.float32)
        edge_index = jax.random.randint(ks[1], (2, N_EDGES), 0, N_NODES, dtype=jnp.int64)
        psi_w = _linear_init(ks[2], 2 * D, (L, 2 * D, D))
        psi_b = _linear_init(ks[3], 2 * D, (L, D))
        phi_w = _linear_init(ks[4], 2 * D, (L, 2 * D, D))
        phi_b = _linear_init(ks[5], 2 * D, (L, D))
        dp_w = _linear_init(ks[6], D, (D, D))
        dp_b = _linear_init(ks[7], D, (D,))
        return {'x': x, 'edge_index': edge_index, 'psi_w': psi_w, 'psi_b': psi_b, 'phi_w': phi_w, 'phi_b': phi_b, 'dp_w': dp_w, 'dp_b': dp_b}
    _L1_gnn_all = _L1_gnn_setup()
    _L1_gnn_in = {k: v for k, v in _L1_gnn_all.items() if k in ('psi_w', 'psi_b', 'phi_w', 'phi_b', 'dp_w', 'dp_b')}
    del _L1_gnn_all
    return {'x': x, 'src': src, 'dst': dst, 'L0_gnn_W_src': _L0_gnn_in['W_src'], 'L0_gnn_W_dst': _L0_gnn_in['W_dst'], 'L0_gnn_attn': _L0_gnn_in['attn'], 'L0_gnn_W_out': _L0_gnn_in['W_out'], 'L0_gnn_b_out': _L0_gnn_in['b_out'], 'L0_gnn_gamma': _L0_gnn_in['gamma'], 'L0_gnn_beta': _L0_gnn_in['beta'], 'L1_gnn_psi_w': _L1_gnn_in['psi_w'], 'L1_gnn_psi_b': _L1_gnn_in['psi_b'], 'L1_gnn_phi_w': _L1_gnn_in['phi_w'], 'L1_gnn_phi_b': _L1_gnn_in['phi_b'], 'L1_gnn_dp_w': _L1_gnn_in['dp_w'], 'L1_gnn_dp_b': _L1_gnn_in['dp_b']}

def reference(x, src, dst, L0_gnn_W_src, L0_gnn_W_dst, L0_gnn_attn, L0_gnn_W_out, L0_gnn_b_out, L0_gnn_gamma, L0_gnn_beta, L1_gnn_psi_w, L1_gnn_psi_b, L1_gnn_phi_w, L1_gnn_phi_b, L1_gnn_dp_w, L1_gnn_dp_b):
    import jax
    import jax.numpy as jnp

    def _L0_gnn_ref(x, edge_index, W_src, W_dst, attn, W_out, b_out, gamma, beta):
        import jax, jax.numpy as jnp
        import numpy as np
        N_NODES = 50000
        N_EDGES = 25000
        IN_DIM = 128
        OUT_DIM = 128
        NUM_HEADS = 8
        HEAD_DIM = OUT_DIM // NUM_HEADS
        LN_EPS = 1e-05
        N = x.shape[0]
        H, D = attn.shape
        src, dst = (edge_index[0], edge_index[1])
        h_src = (x @ W_src).reshape(N, H, D)
        h_dst = (x @ W_dst).reshape(N, H, D)
        h_src_e = h_src[src]
        e = jax.nn.leaky_relu(h_src_e + h_dst[dst], 0.2)
        s = jnp.einsum('ehd,hd->eh', e, attn)
        m = jax.ops.segment_max(s, dst, num_segments=N)
        exp = jnp.exp(s - m[dst])
        denom = jax.ops.segment_sum(exp, dst, num_segments=N)
        alpha = exp / (denom[dst] + 1e-08)
        msg = (h_src_e * alpha[..., None]).reshape(-1, H * D)
        out = jax.ops.segment_sum(msg, dst, num_segments=N)
        out = out @ W_out + b_out
        out = out + x
        mu = jnp.mean(out, axis=-1, keepdims=True)
        var = jnp.var(out, axis=-1, keepdims=True)
        out = (out - mu) * jax.lax.rsqrt(var + LN_EPS) * gamma + beta
        return out

    def _L1_gnn_ref(x, edge_index, psi_w, psi_b, phi_w, phi_b, dp_w, dp_b):
        import jax, jax.numpy as jnp
        import numpy as np
        N_NODES = 1250
        N_EDGES = 20000
        D = 128
        L = 3

        def _linear_init(key, fan_in, shape):
            s = 1.0 / np.sqrt(fan_in)
            return jax.random.uniform(key, shape, minval=-s, maxval=s, dtype=jnp.float32)
        src = edge_index[0]
        dst = edge_index[1]
        n = x.shape[0]
        deg = jax.ops.segment_sum(jnp.ones((src.shape[0],), dtype=x.dtype), dst, num_segments=n)
        inv_deg = (1.0 / jnp.maximum(deg, 1.0))[:, None]
        for l in range(L):
            m = jax.nn.relu(jnp.concatenate([x[dst], x[src]], axis=-1) @ psi_w[l] + psi_b[l])
            agg = jax.ops.segment_sum(m, dst, num_segments=n) * inv_deg
            x = jax.nn.relu(jnp.concatenate([x, agg], axis=-1) @ phi_w[l] + phi_b[l]) + x
        return x @ dp_w + dp_b
    edge_index = jnp.stack([src, dst])
    x = _layernorm(x + _L0_gnn_ref(x, edge_index, L0_gnn_W_src, L0_gnn_W_dst, L0_gnn_attn, L0_gnn_W_out, L0_gnn_b_out, L0_gnn_gamma, L0_gnn_beta), axis=-1)
    x = _layernorm(x + _L1_gnn_ref(x, edge_index, L1_gnn_psi_w, L1_gnn_psi_b, L1_gnn_phi_w, L1_gnn_phi_b, L1_gnn_dp_w, L1_gnn_dp_b), axis=-1)
    return x

_drawn_inputs = setup_inputs


def setup_inputs(seed=0):
    import zlib

    import numpy as np

    out = dict(_drawn_inputs(seed))
    spreads = {'L0_gnn_b_out': (0.0, 0.1), 'L0_gnn_gamma': (1.0, 0.2), 'L0_gnn_beta': (0.0, 0.1)}
    factors = {'L1_gnn_psi_b': 8.0}
    for name, (base, spread) in spreads.items():
        noise = np.random.default_rng([zlib.crc32(name.encode()), seed]).standard_normal(out[name].shape)
        drawn = base * np.exp(spread * noise) if base else spread * noise
        out[name] = jnp.asarray(drawn.astype(out[name].dtype))
    for name, factor in factors.items():
        out[name] = (out[name] * factor).astype(out[name].dtype)
    return out
```

```python
import concourse.bass as bass
from concourse import mybir
from contextlib import ExitStack

FP32 = mybir.dt.float32
I32 = mybir.dt.int32
ALU = mybir.AluOpType
ACT = mybir.ActivationFunctionType
AXIS = mybir.AxisListType

N = 50000
E = 50000
D = 128
H = 8
HD = D // H
NB = 80
SLOTS = 128
NBLK = N // NB
K = 5
BATCHES = NBLK // K
BN = K * NB
BS = K * SLOTS
UNROLL = 4
TP, TT = 125, 4
TN = TP * TT
TILES = N // TN
LAYERS = 3
EPS = 1e-5
BIG = 1e30
GP = 125
GG = NBLK // GP
EROWS = 392
QN = 25
EC = E // GP


class At:

    def __init__(self, turn, off, count):
        self.turn, self.off, self.count = turn, off, count
        self.fixed = isinstance(turn, int)

    def back(self, lag):
        return At(self.turn, self.off - lag, self.count)

    def live(self):
        return not self.fixed or 0 <= UNROLL * self.turn + self.off < self.count

    def n(self, plus=0, times=1):
        return self.turn * (UNROLL * times) + (self.off + plus) * times

    def slot(self, slots):
        return self.off % slots

    def use(self, slots, plus=0):
        return self.turn * (UNROLL // slots) + self.off // slots + plus


def walk(eng, body, count, lag):
    for off in range(UNROLL):
        body(At(0, off, count))
    turns = count // UNROLL
    with eng.Fori(1, turns) as turn:
        for off in range(UNROLL):
            body(At(turn, off, count))
    for off in range(count % UNROLL + lag):
        body(At(0, turns * UNROLL + off, count))


def wait(eng, sem, value):
    if not isinstance(value, int) or value > 0:
        eng.wait_ge(sem, value)


def gnn_kernel(nc, xT, x, src_dst, dst_cols, src_flat, dst_pad, w_src, w_dst, attn, w_out, b_out, gamma, beta,
               psi_dst, psi_src, psi_b, phi_x, phi_agg, phi_b, dp_w, dp_b, out):
    ctx = ExitStack()
    with ctx:
        scope = [ctx]

        def sb(name, shape, dt=FP32):
            return scope[-1].enter_context(nc.sbuf_tensor(name, shape, dt))

        def own_space():
            scope.append(ExitStack())

        def give_back():
            scope.pop().close()

        def sem(name):
            return ctx.enter_context(nc.semaphore(name))

        def dram(name, shape, dt=FP32):
            return nc.dram_tensor(name, shape, dt, kind="Internal").ap()

        hs_table = dram("hs_table", [N, D])
        attT = dram("attT", [D, N])
        resid_rows = dram("resid_rows", [N, D])
        xT_l = [dram(f"xT_{l}", [D, N]) for l in range(LAYERS)]
        y_table = [dram(f"y_table_{l}", [N, D]) for l in range(LAYERS)]
        masks_d = dram("masks_d", [NBLK, 4, SLOTS])
        dloc_d = dram("dloc_d", [NBLK, SLOTS])
        start_d = dram("start_d", [QN, QN])

        ident = sb("ident", [128, 128])
        iota_row = sb("iota_row", [128, 128])
        iota_col = sb("iota_col", [128, 1])
        eps_col = sb("eps_col", [128, 1])
        ones_row = sb("ones_row", [1, 128])
        iota_i = sb("iota_i", [128, 128], I32)
        iota_ci = sb("iota_ci", [128, 1], I32)
        w_src_s = sb("w_src_s", [D, D])
        w_dst_s = sb("w_dst_s", [D, D])
        w_out_s = sb("w_out_s", [D, D])
        dp_s = sb("dp_s", [D, D])
        psi_dst_s = sb("psi_dst_s", [D, LAYERS, D])
        psi_src_s = sb("psi_src_s", [D, LAYERS, D])
        phi_x_s = sb("phi_x_s", [D, LAYERS, D])
        phi_agg_s = sb("phi_agg_s", [D, LAYERS, D])
        psi_b_bc = sb("psi_b_bc", [128, LAYERS, D])
        phi_b_col = sb("phi_b_col", [D, LAYERS])
        attn_bc = sb("attn_bc", [128, D])
        gamma_bc = sb("gamma_bc", [128, D])
        beta_bc = sb("beta_bc", [128, D])
        bout_bc = sb("bout_bc", [128, D])
        dpb_bc = sb("dpb_bc", [128, D])

        dloc_c = sb("dloc_c", [SLOTS, NBLK])
        invdeg_c = sb("invdeg_c", [SLOTS, NBLK])
        src_c = sb("src_c", [SLOTS, NBLK], I32)

        fits_i = sb("fits_i", [1, 1], I32)

        bank = [ctx.enter_context(nc.psum_tensor(f"bank{i}", [128, 512], FP32)) for i in range(4)]
        wide = [ctx.enter_context(nc.psum_tensor(f"wide{i}", [128, 1024], FP32)) for i in range(2)]

        phase_done = sem("phase_done")
        const_in = sem("const_in")
        iota_made = sem("iota_made")
        const_made = sem("const_made")
        CONSTS = 18

        waits_apart = sem("waits_apart")

        def apart(eng):
            eng.sem_inc(waits_apart, 1)

        def flat(ap):
            return ap.rearrange("p t d -> p (t d)")

        def begin(eng, phases):
            if phases:
                eng.wait_ge(phase_done, phases)

        own_space()
        dst_i = sb("dst_i", [GP, EC], I32)
        dst_f = sb("dst_f", [GP, EC])
        quot = sb("quot", [GP, EC])
        resid = sb("resid", [GP, EC])
        is_q = sb("is_q", [GP, EC, QN], mybir.dt.bfloat16)
        is_below = sb("is_below", [GP, EC, QN + 1], mybir.dt.bfloat16)
        counts = sb("counts", [QN, QN + 1])
        upper = sb("upper", [QN, QN])
        start_q = sb("start_q", [QN, QN])
        filled = sb("filled", [QN, QN])
        fullest = sb("fullest", [QN, 1])
        fullest_row = sb("fullest_row", [1, 1])
        fits_f = sb("fits_f", [1, 1])
        start_s = sb("start_s", [GP, GG])
        start_i = sb("start_i", [GP, GG], I32)
        row_i = sb("row_i", [GP, 2, GG], I32)
        rot_i = sb("rot_i", [GP, GG], I32)
        bit_i = sb("bit_i", [GP, 7, GG], I32)
        bit_f = sb("bit_f", [GP, 7, GG, 2])
        win_i = sb("win_i", [GP, GG, 2, 2, SLOTS], I32)
        win = [sb(f"win{i}", [GP, GG, 2, 2 * SLOTS]) for i in range(2)]
        step = sb("step", [GP, GG, 2, 2 * SLOTS])
        base_i = sb("base_i", [GP, GG], I32)
        base_f = sb("base_f", [GP, GG])
        dloc_r = sb("dloc_r", [GP, GG, SLOTS])
        src_r = sb("src_r", [GP, GG, SLOTS])
        masks = sb("masks", [GP, GG, 4, SLOTS])
        ones_r = sb("ones_r", [GP, SLOTS])
        cnt_f = sb("cnt_f", [GP, GG, SLOTS])
        deg_r = sb("deg_r", [GP, GG, SLOTS])
        invdeg_r = sb("invdeg_r", [GP, GG, SLOTS])

        dst_in = sem("dst_in")
        hot_ready = sem("hot_ready")
        count_done = sem("count_done")
        counts_ready = sem("counts_ready")
        base_done = sem("base_done")
        start_ready = sem("start_ready")
        start_out = sem("start_out")
        start_in = sem("start_in")
        rows_ready = sem("rows_ready")
        win_in = sem("win_in")
        tables_ready = sem("tables_ready")
        tables_out = sem("tables_out")
        col_done = sem("col_done")
        col_free = sem("col_free")
        prep_link = sem("prep_link")
        fullest_ready = sem("fullest_ready")
        fullest_turned = sem("fullest_turned")
        fits_ready = sem("fits_ready")

        def prep_sync(sp):
            sp.dma_start(dst_i[:], dst_cols).then_inc(dst_in, 16)
            for tile, source in ((w_src_s, w_src), (w_dst_s, w_dst), (w_out_s, w_out), (dp_s, dp_w)):
                sp.dma_start(tile[:], source).then_inc(const_in, 16)
            for tile, source in ((psi_dst_s, psi_dst), (psi_src_s, psi_src), (phi_x_s, phi_x), (phi_agg_s, phi_agg)):
                for l in range(LAYERS):
                    sp.dma_start(tile[:, l, :], source[l]).then_inc(const_in, 16 if l < LAYERS - 1 else 16)
            for l in range(LAYERS):
                sp.dma_start(psi_b_bc[:, l, :], psi_b[l:l + 1, :].partition_broadcast(128)).then_inc(const_in, 16)
            sp.dma_start(phi_b_col[:], phi_b).then_inc(const_in, 16)
            for tile, source in ((attn_bc, attn), (gamma_bc, gamma), (beta_bc, beta), (bout_bc, b_out), (dpb_bc, dp_b)):
                sp.dma_start(tile[:], source.partition_broadcast(128)).then_inc(const_in, 16)
            sp.wait_ge(const_in, 16 * (4 + 4 * LAYERS + LAYERS + 1 + 5))
            sp.wait_ge(start_ready, 1)
            sp.dma_start(start_d, start_q[:]).then_inc(start_out, 16)
            sp.wait_ge(start_out, 16)
            sp.dma_start(start_s[:], start_d.rearrange("q r -> (q r)").rearrange("(p g) -> p g", g=GG)).then_inc(start_in, 16)
            sp.wait_ge(tables_ready, 1)
            sp.dma_start(masks_d.rearrange("(p g) m s -> p (g m s)", g=GG), masks[:].rearrange("p g m s -> p (g m s)")).then_inc(tables_out, 16)
            sp.dma_start(dloc_d.rearrange("(p g) s -> p (g s)", g=GG), dloc_r[:].rearrange("p g s -> p (g s)")).then_inc(tables_out, 16)
            sp.wait_ge(tables_out, 32)
            sp.wait_ge(col_free, 3 * GG)

        def prep_gpsimd(pool):
            nc.gpsimd.iota(iota_i[:], [[1, 128]], 0, 0).then_inc(iota_made, 1)
            nc.gpsimd.iota(iota_ci[:], [[0, 1]], 0, 1).then_inc(iota_made, 1)
            nc.gpsimd.iota(base_i[:], [[NB, GG]], 0, NB * GG).then_inc(iota_made, 1)
            pool.wait_ge(rows_ready, 1)
            for g in range(GG):
                for r in range(2):
                    nc.gpsimd.indirect_dma_start(
                        win_i[:, g, r, :, :].rearrange("p k s -> p (k s)"), None, src_dst,
                        bass.IndirectOffsetOnAxis(ap=row_i[:, r, g:g + 1], axis=0)).then_inc(win_in, 16)

        def prep_vector(dve):
            made = [0]

            def link(ins):
                made[0] += 1
                ins.then_inc(prep_link, 1)
                dve.wait_ge(prep_link, made[0])

            v = nc.vector
            dve.wait_ge(iota_made, 3)
            link(v.tensor_copy(iota_row[:], iota_i[:]))
            link(v.tensor_copy(iota_col[:], iota_ci[:]))
            link(v.memset(eps_col[:], EPS))
            link(v.memset(ones_row[:], 1.0))
            link(v.tensor_copy(base_f[:], base_i[:]))
            v.tensor_scalar(ident[:], iota_row[:], iota_col[:, 0:1], None, ALU.is_equal).then_inc(const_made, 1)
            link(v.tensor_scalar(upper[:], iota_row[0:QN, 0:QN], iota_col[0:QN, 0:1], None, ALU.is_gt))
            dve.wait_ge(dst_in, 16)
            link(v.tensor_copy(dst_f[:], dst_i[:]))
            link(v.tensor_scalar(quot[:], dst_f[:], float(NB * QN), None, ALU.is_ge))
            for q in range(2, QN):
                link(v.scalar_tensor_tensor(quot[:], dst_f[:], float(NB * QN * q), quot[:], ALU.is_ge, ALU.add))
            link(v.scalar_tensor_tensor(resid[:], quot[:], -float(NB * QN), dst_f[:], ALU.mult, ALU.add))
            link(v.tensor_scalar(resid[:], resid[:], 1.0 / NB, None, ALU.mult))
            link(v.tensor_tensor(is_q[:], quot[:].unsqueeze(2).broadcast_to([GP, EC, QN]),
                                 iota_row[0:GP, 0:QN].unsqueeze(1).broadcast_to([GP, EC, QN]), ALU.is_equal))
            v.tensor_tensor(is_below[:], resid[:].unsqueeze(2).broadcast_to([GP, EC, QN + 1]),
                            iota_row[0:GP, 0:QN + 1].unsqueeze(1).broadcast_to([GP, EC, QN + 1]),
                            ALU.is_lt).then_inc(hot_ready, 1)
            dve.wait_ge(count_done, 1)
            v.tensor_copy(counts[:], bank[0][0:QN, 0:QN + 1]).then_inc(counts_ready, 1)
            dve.wait_ge(counts_ready, 1)
            dve.wait_ge(base_done, 1)
            v.tensor_scalar(start_q[:], counts[:, 0:QN], bank[1][0:QN, 0:1], None, ALU.add).then_inc(start_ready, 1)
            link(v.tensor_tensor(filled[:], counts[:, 1:QN + 1], counts[:, 0:QN], ALU.subtract))
            v.tensor_reduce(fullest[:], filled[:], AXIS.X, ALU.max).then_inc(fullest_ready, 1)
            dve.wait_ge(fullest_turned, 1)
            link(v.tensor_reduce(fullest_row[:], bank[2][0:1, 0:QN], AXIS.X, ALU.max))
            link(v.tensor_scalar(fits_f[:], fullest_row[:], float(SLOTS), None, ALU.is_le))
            v.tensor_copy(fits_i[:], fits_f[:]).then_inc(fits_ready, 1)
            dve.wait_ge(start_in, 16)
            link(v.tensor_copy(start_i[:], start_s[:]))
            link(v.tensor_scalar(row_i[:, 0, :], start_i[:], 7, None, ALU.logical_shift_right))
            link(v.tensor_scalar(rot_i[:], start_i[:], SLOTS - 1, None, ALU.bitwise_and))
            v.tensor_scalar(row_i[:, 1, :], row_i[:, 0, :], 1, None, ALU.add).then_inc(rows_ready, 1)
            for b in range(7):
                link(v.tensor_scalar(bit_i[:, b, :], rot_i[:], b, 1, ALU.logical_shift_right, ALU.bitwise_and))
            link(v.tensor_copy(bit_f[:], bit_i[:].unsqueeze(3).broadcast_to([GP, 7, GG, 2])))
            dve.wait_ge(win_in, 16 * 2 * GG)
            for r in range(2):
                link(v.tensor_copy(win[0][:, :, :, r * SLOTS:(r + 1) * SLOTS], win_i[:, :, r, :, :]))
            left, at = 2 * SLOTS, 0
            for b in range(6, -1, -1):
                left -= 1 << b
                now = win[at][:].rearrange("p g k s -> p (g k) s")
                new = win[1 - at][:].rearrange("p g k s -> p (g k) s")
                dif = step[:].rearrange("p g k s -> p (g k) s")[:, :, 0:left]
                bits = bit_f[:, b, :, :].rearrange("p g k -> p (g k)").unsqueeze(2).broadcast_to([GP, 2 * GG, left])
                link(v.tensor_tensor(dif, now[:, :, (1 << b):(1 << b) + left], now[:, :, 0:left], ALU.subtract))
                link(v.tensor_tensor(dif, dif, bits, ALU.mult))
                link(v.tensor_tensor(new[:, :, 0:left], dif, now[:, :, 0:left], ALU.add))
                at = 1 - at
            src_w, dst_w = win[at][:, :, 0, 0:SLOTS], win[at][:, :, 1, 0:SLOTS]
            link(v.tensor_copy(src_r[:], src_w))
            link(v.tensor_tensor(dloc_r[:], dst_w, base_f[:].unsqueeze(2).broadcast_to([GP, GG, SLOTS]), ALU.subtract))
            link(v.memset(masks[:], 0.0))
            link(v.memset(ones_r[:], 1.0))
            link(v.tensor_tensor(masks[:, :, 2, 1:], dloc_r[:, :, 1:], dloc_r[:, :, 0:SLOTS - 1], ALU.is_equal))
            link(v.tensor_tensor(masks[:, :, 3, 0:SLOTS - 1], dloc_r[:, :, 1:], dloc_r[:, :, 0:SLOTS - 1], ALU.is_equal))
            link(v.tensor_scalar(masks[:, :, 0:2, :], masks[:, :, 2:4, :], BIG, -BIG, ALU.mult, ALU.add))
            for g in range(GG):
                link(v.tensor_tensor_scan(cnt_f[:, g, :], masks[:, g, 2, :], ones_r[:], 0.0, ALU.mult, ALU.add))
                link(v.tensor_tensor_scan(deg_r[:, g, ::-1], masks[:, g, 3, ::-1], cnt_f[:, g, ::-1], 0.0, ALU.mult, ALU.max))
            v.reciprocal(invdeg_r[:], deg_r[:]).then_inc(tables_ready, 1)
            n = 0
            for g in range(GG):
                for table in (dloc_c, invdeg_c, src_c):
                    dve.wait_ge(col_done, n + 1)
                    v.tensor_copy(table[:, g::GG], bank[2 + n % 2][:, 0:GP]).then_inc(col_free, 1)
                    n += 1

        def prep_tensor(pe):
            pe.wait_ge(hot_ready, 1)
            for c in range(EC):
                last = nc.tensor.matmul(bank[0][0:QN, 0:QN + 1], is_q[:, c, :], is_below[:, c, :],
                                        start=(c == 0), stop=(c == EC - 1))
            last.then_inc(count_done, 1)
            pe.wait_ge(counts_ready, 1)
            nc.tensor.matmul(bank[1][0:QN, 0:1], upper[:], counts[:, QN:QN + 1], start=True, stop=True).then_inc(base_done, 1)
            pe.wait_ge(fullest_ready, 1)
            pe.wait_ge(const_made, 1)
            nc.tensor.transpose(bank[2][0:1, 0:QN], fullest[:], ident[0:QN, 0:QN]).then_inc(fullest_turned, 1)
            pe.wait_ge(tables_ready, 1)
            n = 0
            for g in range(GG):
                for table in (dloc_r, invdeg_r, src_r):
                    wait(pe, col_free, n - 1)
                    nc.tensor.transpose(bank[2 + n % 2][:, 0:GP], table[:, g, :], ident[0:GP, 0:GP]).then_inc(col_done, 1)
                    n += 1

        give_back()
        own_space()
        xt_in = sb("xt_in", [D, UNROLL, TN])
        hs_out = sb("hs_out", [TP, UNROLL, TT, D])
        t_in = [sem(f"t_in{s}") for s in range(UNROLL)]
        t_out = [sem(f"t_out{s}") for s in range(UNROLL)]
        t_mm = sem("t_mm")
        t_ev = sem("t_ev")

        def rows_of(table, i):
            return table[bass.ds(i.n(0, TN), TN), :].rearrange("(t p) d -> p t d", p=TP)

        def table_sync(sp):
            def body(i):
                if i.live():
                    wait(sp, t_mm, i.n(1 - UNROLL))
                    sp.dma_start(xt_in[:, i.slot(4), :], xT[:, bass.ds(i.n(0, TN), TN)]).then_inc(t_in[i.slot(4)], 16)
                k = i.back(2)
                if k.live():
                    sp.wait_ge(t_ev, k.n(1))
                    sp.dma_start(rows_of(hs_table, k), hs_out[:, k.slot(4), :, :]).then_inc(t_out[k.slot(4)], 16)
            walk(sp, body, TILES, 2)
            for s in range(UNROLL):
                sp.wait_ge(t_out[s], 16 * len(range(s, TILES, UNROLL)))

        def table_tensor(pe):
            def body(i):
                if i.live():
                    pe.wait_ge(t_in[i.slot(4)], i.use(4, 1) * 16)
                    wait(pe, t_ev, i.n(-1))
                    for t in range(TT):
                        last = nc.tensor.matmul(bank[i.slot(2)][0:TP, t * D:(t + 1) * D],
                                                xt_in[:, i.slot(4), t * TP:(t + 1) * TP], w_src_s[:], start=True, stop=True)
                    last.then_inc(t_mm, 1)
            walk(pe, body, TILES, 0)

        def table_scalar(act):
            def body(i):
                if i.live():
                    act.wait_ge(t_mm, i.n(1))
                    wait(act, t_out[i.slot(4)], i.use(4) * 16)
                    nc.scalar.copy(hs_out[:, i.slot(4), :, :].rearrange("p t d -> p (t d)"),
                                   bank[i.slot(2)][0:TP, :]).then_inc(t_ev, 1)
            walk(act, body, TILES, 0)

        give_back()

        own_space()
        o_in = sb("o_in", [D, TN])
        o_rows = sb("o_rows", [TP, TT, D])
        o_resid = sb("o_resid", [TP, TT, D])
        o_T = sb("o_T", [D, TN])
        o_agg = sb("o_agg", [D, TN])
        o_st = sb("o_st", [TP, TT, 6])
        o_mv = sb("o_mv", [TP, 1, TT, 2])
        o_log = sb("o_log", [TP, 1, TT])
        o_rs = sb("o_rs", [TP, 1, TT])
        o_sh = sb("o_sh", [TP, 1, TT])
        e_src = sb("e_src", [TP, 1], I32)
        e_ints = sb("e_ints", [TP, 3], I32)
        e_row_i = sb("e_row_i", [TP, 2, TP], I32)
        e_cols = sb("e_cols", [TP, 3])
        e_row = sb("e_row", [TP, 2, TP])
        e_more = sb("e_more", [TP, 1])
        e_put_f = sb("e_put_f", [TP, 1])
        e_put = sb("e_put", [TP, 1], I32)
        is_last = sb("is_last", [TP, 1])
        same = sb("same", [TP, TP])
        carry_on = sb("carry_on", [TP, TP])
        src_rows = sb("src_rows", [TP, D])
        dst_rows = sb("dst_rows", [TP, D])
        max_rows = sb("max_rows", [TP, H])
        e_pre = sb("e_pre", [TP, D])
        e_leaky = sb("e_leaky", [TP, D])
        e_prod = sb("e_prod", [TP, D])
        e_score = sb("e_score", [TP, H])
        e_keep = sb("e_keep", [H, TP])
        e_pen = sb("e_pen", [H, TP])
        e_sT = sb("e_sT", [H, TP])
        e_run = sb("e_run", [H, TP])
        e_last = sb("e_last", [H, 1])
        e_shift = sb("e_shift", [TP, H])
        e_max = sb("e_max", [TP, H])
        e_terms = sb("e_terms", [TP, D + H])
        e_total = sb("e_total", [TP, D + H])
        e_den = sb("e_den", [TP, H])
        e_inv = sb("e_inv", [TP, H])
        e_out = sb("e_out", [TP, D])
        give_back()

        g_x = [sem(f"g_x{s}") for s in range(UNROLL)]
        g_dl = [sem(f"g_dl{s}") for s in range(2)]
        g_rows = [sem(f"g_rows{s}") for s in range(UNROLL)]
        g_xo = [sem(f"g_xo{s}") for s in range(UNROLL)]
        g_yo = [sem(f"g_yo{s}") for s in range(UNROLL)]
        g_x1 = [sem(f"g_resid{s}") for s in range(2)]
        (g_idx, g_slot1h, g_node1h, g_z, g_zev, g_u, g_pre, g_m, g_agg, g_aggev, g_q, g_relu, g_xnew, g_y, g_yev,
         f_sum, f_st, f_mv, f_log, f_rstd, f_sh) = [sem(s) for s in (
             "g_idx", "g_slot1h", "g_node1h", "g_z", "g_zev", "g_u", "g_pre", "g_m", "g_agg", "g_aggev", "g_q", "g_relu", "g_xnew",
             "g_y", "g_yev", "f_sum", "f_st", "f_mv", "f_log", "f_rstd", "f_sh")]
        paired = iter([g_idx, g_slot1h, g_node1h, g_z, g_zev, g_u, g_pre, g_m, g_agg, g_aggev, g_q, g_relu, g_xnew, g_y, g_yev,
                       f_sum, f_st, f_mv, f_log, f_rstd, f_sh, *g_xo, *g_yo])
        name_of = {}

        def twin(name):
            handle = next(paired)
            name_of[handle.num] = name
            return handle

        o_loaded, o_product, o_copied, o_stored, o_relu, o_sum, o_stat, o_mvs, o_logs, o_rstd, o_shs = [twin(s) for s in (
            "o_loaded", "o_product", "o_copied", "o_stored", "o_relu", "o_sum", "o_stat", "o_mvs", "o_logs", "o_rstd", "o_shs")]
        e_loaded, e_gathered, e_indexed, e_link, e_scored, e_terms_in, e_turned, e_ran, e_shifted, e_probs, e_result, e_scattered, e_kept = [
            twin(s) for s in ("e_loaded", "e_gathered", "e_indexed", "e_link", "e_scored", "e_terms_in", "e_turned", "e_ran",
                             "e_shifted", "e_probs", "e_result", "e_scattered", "e_kept")]
        zero_made = sem("zero_made")
        zero_out = sem("zero_out")

        hd_table = dram("hd_table", [N, D])
        max_table = dram("max_table", [N, H])
        score_d = dram("score_d", [E, H])
        att_rows = dram("att_rows", [N, D])
        agg_rows = dram("agg_rows", [N, D])
        aggT_d = dram("aggT_d", [D, N])
        fin_rows = dram("fin_rows", [N, D])
        xT_last = dram("xT_last", [D, N])

        def tile_rows(table, t):
            return table[bass.ds(t * TN, TN), :].rearrange("(t p) d -> p t d", p=TP)

        def tile_cols(table, t):
            return table[:, bass.ds(t * TN, TN)]

        NODE_RATES = {
            "table": {"o_loaded": 16, "o_product": 1, "o_copied": 1, "o_stored": 16},
            "turn": {"o_loaded": 16, "o_product": 1, "o_copied": 1, "o_stored": 16},
            "update": {"o_loaded": 32, "o_product": 1, "o_relu": 1, "o_copied": 1, "o_stored": 16},
            "final": {"o_loaded": 32, "o_sum": 1, "o_stat": 1, "o_mvs": 1, "o_logs": 1, "o_rstd": 1, "o_shs": 1,
                      "o_copied": 1, "o_stored": 16},
        }
        LINKS = {"scores": 11, "attend": 9, "mean": 9}
        EDGE_RATES = {
            "scores": {"e_loaded": 96, "e_gathered": 32, "e_indexed": 1, "e_link": LINKS["scores"], "e_scored": 1, "e_turned": 2,
                       "e_ran": 1, "e_result": 1, "e_scattered": 16, "e_kept": 16},
            "attend": {"e_loaded": 112, "e_gathered": 32, "e_indexed": 1, "e_link": LINKS["attend"], "e_shifted": 1, "e_probs": 1,
                       "e_terms_in": 1, "e_turned": 1, "e_result": 1, "e_scattered": 16},
            "mean": {"e_loaded": 96, "e_gathered": 32, "e_indexed": 1, "e_link": LINKS["mean"], "e_terms_in": 1, "e_turned": 1,
                     "e_result": 1, "e_scattered": 16},
        }

        def counted(plan, at):
            tiles = {**{k: TILES for k in NODE_RATES}, **{k: EC for k in EDGE_RATES}}
            rates = {**NODE_RATES, **EDGE_RATES}

            def after(s, t, k):
                base = sum(rates[p[0]].get(name_of[s.num], 0) * tiles[p[0]] for p in plan[:at])
                return t * rates[plan[at][0]][name_of[s.num]] + (base + k)
            return after

        def node_sync(sp, after, kind, source, dest, second=None, **_):
            with sp.Fori(0, TILES) as t:
                if kind in ("table", "update"):
                    sp.dma_start(o_in[:], tile_cols(source, t)).then_inc(o_loaded, 16)
                else:
                    sp.dma_start(o_rows[:], tile_rows(source, t)).then_inc(o_loaded, 16)
                if kind == "update":
                    sp.dma_start(o_agg[:], tile_cols(second, t)).then_inc(o_loaded, 16)
                if kind == "final":
                    sp.dma_start(o_resid[:], tile_rows(second, t)).then_inc(o_loaded, 16)
                sp.wait_ge(o_copied, after(o_copied, t, 1))
                apart(sp)
                if kind in ("table", "final"):
                    sp.dma_start(tile_rows(dest, t), o_rows[:]).then_inc(o_stored, 16)
                else:
                    sp.dma_start(tile_cols(dest, t), o_T[:]).then_inc(o_stored, 16)
                sp.wait_ge(o_stored, after(o_stored, t, 16))
                apart(sp)

        def node_tensor(pe, after, kind, weight=None, l=0, **_):
            if kind == "final":
                return
            with pe.Fori(0, TILES) as t:
                pe.wait_ge(o_loaded, after(o_loaded, t, NODE_RATES[kind]["o_loaded"]))
                apart(pe)
                if kind == "table":
                    for c in range(TT):
                        last = nc.tensor.matmul(bank[0][0:TP, c * D:(c + 1) * D], o_in[:, c * TP:(c + 1) * TP], weight, start=True, stop=True)
                elif kind == "turn":
                    for c in range(TT):
                        last = nc.tensor.transpose(bank[0][:, c * TP:(c + 1) * TP], o_rows[:, c, :], ident[0:TP, 0:TP])
                else:
                    nc.tensor.matmul(bank[0][:, 0:TN], phi_x_s[:, l, :], o_in[:], start=True, stop=False)
                    last = nc.tensor.matmul(bank[0][:, 0:TN], phi_agg_s[:, l, :], o_agg[:], start=False, stop=True)
                last.then_inc(o_product, 1)

        def node_scalar(act, after, kind, l=0, **_):
            if kind not in ("update", "final"):
                return
            with act.Fori(0, TILES) as t:
                if kind == "update":
                    act.wait_ge(o_product, after(o_product, t, 1))
                    nc.scalar.activation(o_T[:], bank[0][:, 0:TN], ACT.Relu, bias=phi_b_col[:, l:l + 1]).then_inc(o_relu, 1)
                else:
                    act.wait_ge(o_mvs, after(o_mvs, t, 1))
                    nc.scalar.activation(o_log[:, 0, :], o_mv[:, 0, :, 1], ACT.Ln, bias=eps_col[0:TP, 0:1]).then_inc(o_logs, 1)
                    act.wait_ge(o_logs, after(o_logs, t, 1))
                    nc.scalar.activation(o_rs[:, 0, :], o_log[:, 0, :], ACT.Exp, scale=-0.5).then_inc(o_rstd, 1)
                    act.wait_ge(o_shs, after(o_shs, t, 1))
                    for c in range(TT):
                        last = nc.scalar.activation(o_rows[:, c, :], o_resid[:, c, :], ACT.Identity,
                                                    bias=o_sh[:, 0, c:c + 1], scale=o_rs[:, 0, c:c + 1])
                    last.then_inc(o_copied, 1)

        def node_vector(dve, after, kind, bias=None, **_):
            v = nc.vector
            with dve.Fori(0, TILES) as t:
                if kind == "table":
                    dve.wait_ge(o_product, after(o_product, t, 1))
                    if bias is None:
                        v.tensor_copy(flat(o_rows[:]), bank[0][0:TP, :]).then_inc(o_copied, 1)
                    else:
                        v.tensor_tensor(o_rows[:], bank[0][0:TP, :].rearrange("p (t d) -> p t d", d=D),
                                        bias.unsqueeze(1).broadcast_to([TP, TT, D]), ALU.add).then_inc(o_copied, 1)
                elif kind == "turn":
                    dve.wait_ge(o_product, after(o_product, t, 1))
                    v.tensor_copy(o_T[:], bank[0][:, 0:TN]).then_inc(o_copied, 1)
                elif kind == "update":
                    dve.wait_ge(o_relu, after(o_relu, t, 1))
                    v.tensor_tensor(o_T[:], o_T[:], o_in[:], ALU.add).then_inc(o_copied, 1)
                else:
                    dve.wait_ge(o_loaded, after(o_loaded, t, 32))
                    v.tensor_tensor(o_resid[:], o_resid[:], o_rows[:], ALU.add).then_inc(o_sum, 1)
                    dve.wait_ge(o_sum, after(o_sum, t, 1))
                    for c in range(TT):
                        last = v.bn_stats(o_st[:, c, :], o_resid[:, c, :])
                    last.then_inc(o_stat, 1)
                    dve.wait_ge(o_stat, after(o_stat, t, 1))
                    apart(dve)
                    for c in range(TT):
                        last = v.bn_aggr(o_mv[:, 0, c, :], o_st[:, c, :])
                    last.then_inc(o_mvs, 1)
                    dve.wait_ge(o_rstd, after(o_rstd, t, 1))
                    v.scalar_tensor_tensor(o_sh[:, 0, :], o_mv[:, 0, :, 0], -1.0, o_rs[:, 0, :], ALU.mult, ALU.mult).then_inc(o_shs, 1)

        def edge_sync(sp, after, kind, **_):
            with sp.Fori(0, EC) as t:
                sp.dma_start(e_src[:], src_flat[bass.ds(t * TP, TP), :]).then_inc(e_loaded, 16)
                sp.dma_start(e_ints[:, 0:1], dst_pad[bass.ds(t * TP + 1, TP), :]).then_inc(e_loaded, 16)
                sp.dma_start(e_ints[:, 1:2], dst_pad[bass.ds(t * TP + 2, TP), :]).then_inc(e_loaded, 16)
                sp.dma_start(e_ints[:, 2:3].unsqueeze(1), dst_pad[bass.ds(t * TP, 1), :].rearrange("a b -> (a b)").partition_broadcast(TP)).then_inc(e_loaded, 16)
                for r in range(2):
                    sp.dma_start(e_row_i[:, r, :].unsqueeze(1), dst_pad[bass.ds(t * TP + (1 - r), TP), :].rearrange("a b -> (a b)").partition_broadcast(TP)
                                 ).then_inc(e_loaded, 16)
                if kind == "attend":
                    sp.dma_start(e_score[:], score_d[bass.ds(t * TP, TP), :]).then_inc(e_loaded, 16)
                if kind == "scores":
                    sp.wait_ge(e_scored, after(e_scored, t, 1))
                    sp.dma_start(score_d[bass.ds(t * TP, TP), :], e_score[:]).then_inc(e_kept, 16)
                    sp.wait_ge(e_kept, after(e_kept, t, 16))
                sp.wait_ge(e_scattered, after(e_scattered, t, 16))
                apart(sp)

        def edge_gpsimd(pool, after, kind, src_table, dst_table, dest):
            with pool.Fori(0, EC) as t:
                pool.wait_ge(e_indexed, after(e_indexed, t, 1))
                apart(pool)
                nc.gpsimd.indirect_dma_start(src_rows[:], None, src_table, bass.IndirectOffsetOnAxis(ap=e_src[:, 0:1], axis=0)).then_inc(e_gathered, 16)
                nc.gpsimd.indirect_dma_start(max_rows[:] if kind == "attend" else dst_rows[:], None, dst_table,
                                             bass.IndirectOffsetOnAxis(ap=e_ints[:, 0:1], axis=0)).then_inc(e_gathered, 16)
                pool.wait_ge(e_result, after(e_result, t, 1))
                apart(pool)
                nc.gpsimd.indirect_dma_start(dest, bass.IndirectOffsetOnAxis(ap=e_put[:, 0:1], axis=0),
                                             e_max[:] if kind == "scores" else e_out[:], None,
                                             bounds_check=N - 1, oob_is_err=False).then_inc(e_scattered, 16)
                pool.wait_ge(e_scattered, after(e_scattered, t, 16))

        def edge_tensor(pe, after, kind, **_):
            w = D + H if kind == "attend" else D + 1
            with pe.Fori(0, EC) as t:
                if kind == "scores":
                    pe.wait_ge(e_scored, after(e_scored, t, 1))
                    apart(pe)
                    nc.tensor.transpose(bank[0][0:H, 0:TP], e_score[:], ident[0:TP, 0:TP]).then_inc(e_turned, 1)
                    pe.wait_ge(e_ran, after(e_ran, t, 1))
                    apart(pe)
                    nc.tensor.transpose(bank[1][0:TP, 0:H], e_run[:], ident[0:H, 0:H]).then_inc(e_turned, 1)
                else:
                    pe.wait_ge(e_terms_in, after(e_terms_in, t, 1))
                    nc.tensor.matmul(bank[0][0:TP, 0:w], same[:], e_terms[:, 0:w], start=True, stop=False)
                    nc.tensor.matmul(bank[0][0:TP, 0:w], carry_on[:], e_total[:, 0:w], start=False, stop=True).then_inc(e_turned, 1)

        def edge_scalar(act, after, kind, **_):
            if kind == "attend":
                with act.Fori(0, EC) as t:
                    act.wait_ge(e_shifted, after(e_shifted, t, 1))
                    nc.scalar.activation(e_terms[:, D:D + H], e_shift[:], ACT.Exp).then_inc(e_probs, 1)

        def edge_vector(dve, after, kind, **_):
            v = nc.vector
            w = D + H if kind == "attend" else D + 1
            if kind == "mean":
                v.memset(e_terms[:, D:D + 1], 1.0)
            with dve.Fori(0, EC) as t:
                done = [0]

                def link(ins):
                    done[0] += 1
                    ins.then_inc(e_link, 1)
                    dve.wait_ge(e_link, after(e_link, t, done[0]))

                dve.wait_ge(e_loaded, after(e_loaded, t, EDGE_RATES[kind]["e_loaded"]))
                link(v.tensor_copy(e_cols[:], e_ints[:]))
                link(v.tensor_copy(e_row[:], e_row_i[:]))
                link(v.tensor_tensor(e_more[:], e_cols[:, 0:1], e_cols[:, 1:2], ALU.is_equal))
                link(v.scalar_tensor_tensor(e_put_f[:], e_more[:], float(1 << 20), e_cols[:, 0:1], ALU.mult, ALU.add))
                v.tensor_copy(e_put[:], e_put_f[:]).then_inc(e_indexed, 1)
                if kind != "scores":
                    link(v.tensor_scalar(same[:], e_row[:, 0, :], e_cols[:, 0:1], None, ALU.is_equal))
                    link(v.tensor_scalar(carry_on[:], e_row[:, 0, :], e_cols[:, 2:3], is_last[:, 0:1], ALU.is_equal, ALU.mult))
                dve.wait_ge(e_gathered, after(e_gathered, t, 32))
                if kind != "attend":
                    link(v.tensor_tensor(e_pre[:], src_rows[:], dst_rows[:], ALU.add))
                if kind == "scores":
                    link(v.scalar_tensor_tensor(e_leaky[:], e_pre[:], 0.2, e_pre[:], ALU.mult, ALU.max))
                    link(v.tensor_tensor(e_prod[:], e_leaky[:], attn_bc[0:TP, :], ALU.mult))
                    v.tensor_reduce(e_score[:], e_prod[:].rearrange("p (h d) -> p h d", d=HD), AXIS.X, ALU.add).then_inc(e_scored, 1)
                    link(v.tensor_tensor(e_keep[:], e_row[0:H, 0, :], e_row[0:H, 1, :], ALU.is_equal))
                    link(v.tensor_scalar(e_pen[:], e_keep[:], BIG, -BIG, ALU.mult, ALU.add))
                    dve.wait_ge(e_turned, after(e_turned, t, 1))
                    link(v.tensor_copy(e_sT[:], bank[0][0:H, 0:TP]))
                    link(v.tensor_tensor_scan(e_run[:], e_pen[:], e_sT[:], e_last[:, 0:1], ALU.add, ALU.max))
                    v.tensor_copy(e_last[:], e_run[:, TP - 1:TP]).then_inc(e_ran, 1)
                    dve.wait_ge(e_turned, after(e_turned, t, 2))
                    v.tensor_copy(e_max[:], bank[1][0:TP, 0:H]).then_inc(e_result, 1)
                if kind == "attend":
                    v.tensor_tensor(e_shift[:], e_score[:], max_rows[:], ALU.subtract).then_inc(e_shifted, 1)
                    dve.wait_ge(e_probs, after(e_probs, t, 1))
                    v.tensor_tensor(e_terms[:, 0:D].rearrange("p (h d) -> p h d", d=HD), src_rows[:].rearrange("p (h d) -> p h d", d=HD),
                                    e_terms[:, D:D + H].unsqueeze(2).broadcast_to([TP, H, HD]), ALU.mult).then_inc(e_terms_in, 1)
                if kind == "mean":
                    v.tensor_scalar(e_terms[:, 0:D], e_pre[:], 0.0, None, ALU.max).then_inc(e_terms_in, 1)
                if kind != "scores":
                    dve.wait_ge(e_turned, after(e_turned, t, 1))
                    link(v.tensor_copy(e_total[:, 0:w], bank[0][0:TP, 0:w]))
                if kind == "attend":
                    link(v.tensor_scalar(e_den[:], e_total[:, D:D + H], 1e-8, None, ALU.add))
                    link(v.reciprocal(e_inv[:], e_den[:]))
                    v.tensor_tensor(e_out[:].rearrange("p (h d) -> p h d", d=HD), e_total[:, 0:D].rearrange("p (h d) -> p h d", d=HD),
                                    e_inv[:].unsqueeze(2).broadcast_to([TP, H, HD]), ALU.mult).then_inc(e_result, 1)
                if kind == "mean":
                    link(v.reciprocal(e_inv[:, 0:1], e_total[:, D:D + 1]))
                    v.tensor_scalar(e_out[:], e_total[:, 0:D], e_inv[:, 0:1], None, ALU.mult).then_inc(e_result, 1)
                assert done[0] == LINKS[kind], (kind, done[0])

        ATTEND = [
            ("table", dict(source=xT, weight=w_dst_s[:], dest=hd_table)),
            ("scores", dict(src_table=hs_table, dst_table=hd_table, dest=max_table)),
            ("attend", dict(src_table=hs_table, dst_table=max_table, dest=att_rows)),
            ("turn", dict(source=att_rows, dest=attT)),
        ]
        LAYER_PLAN = []
        xs = xT_l + [xT_last]
        for l in range(LAYERS):
            LAYER_PLAN += [
                ("table", dict(source=xs[l], weight=psi_dst_s[:, l, :], bias=psi_b_bc[0:TP, l, :], dest=hd_table)),
                ("mean", dict(src_table=y_table[l], dst_table=hd_table, dest=agg_rows)),
                ("turn", dict(source=agg_rows, dest=aggT_d)),
                ("update", dict(source=xs[l], second=aggT_d, l=l, dest=xs[l + 1])),
            ]
            if l < LAYERS - 1:
                LAYER_PLAN += [("table", dict(source=xs[l + 1], weight=psi_src_s[:, l + 1, :], dest=y_table[l + 1]))]
        LAYER_PLAN += [("table", dict(source=xT_last, weight=dp_s[:], dest=fin_rows)),
                       ("final", dict(source=fin_rows, second=resid_rows, dest=out))]
        PLAN = ATTEND + LAYER_PLAN

        def general(eng, node, edge, first, end):
            for at in range(first, end):
                kind, what = PLAN[at]
                program = node if kind in NODE_RATES else edge
                if program:
                    program(eng, counted(PLAN, at), kind, **what)

        def zero_sync(sp):
            sp.wait_ge(zero_made, 1)
            with sp.Fori(0, TILES) as t:
                for table in (att_rows, agg_rows):
                    sp.dma_start(tile_rows(table, t), o_rows[:]).then_inc(zero_out, 16)
                sp.dma_start(tile_rows(max_table, t), o_rows[:, :, 0:H]).then_inc(zero_out, 16)
            sp.wait_ge(zero_out, 16 * 3 * TILES)

        def zero_vector(dve):
            v = nc.vector
            v.memset(e_total[:], 0.0)
            v.memset(e_last[:], -BIG)
            v.tensor_scalar(is_last[:], iota_col[0:TP, :], float(TP - 1), None, ALU.is_equal)
            v.memset(o_rows[:], 0.0).then_inc(zero_made, 1)

        def by_path(eng, fast, slow):
            eng.wait_ge(fits_ready, 1)
            fits = eng.value_load(fits_i[0:1, 0:1], min_val=0, max_val=1)
            with eng.If(fits > 0):
                fast()
            with eng.Else():
                slow()

        xt_b = sb("xt_b", [D, UNROLL, BN])
        dl_b = sb("dl_b", [NB, 2, BS])
        mask_b = sb("mask_b", [K * H, UNROLL, 4, SLOTS])
        idx_b = sb("idx_b", [SLOTS, UNROLL, K], I32)
        rows_b = sb("rows_b", [SLOTS, UNROLL, K, D])
        hd_b = sb("hd_b", [NB, 2, BS])
        to_slot = sb("to_slot", [NB, 2, BS])
        to_node = sb("to_node", [SLOTS, 2, K, NB])
        pre_b = sb("pre_b", [SLOTS, 2, K * D])
        leaky_b = sb("leaky_b", [SLOTS, 2, K * D])
        prod_b = sb("prod_b", [SLOTS, K * D])
        score_b = sb("score_b", [SLOTS, 2, K * H])
        sT = sb("sT", [K * H, SLOTS])
        run_max = sb("run_max", [K * H, SLOTS])
        seg_max = sb("seg_max", [K * H, SLOTS])
        shifted = sb("shifted", [K * H, SLOTS])
        probs = sb("probs", [K * H, SLOTS])
        run_sum = sb("run_sum", [K * H, SLOTS])
        seg_sum = sb("seg_sum", [K * H, SLOTS])
        seg_eps = sb("seg_eps", [K * H, SLOTS])
        seg_inv = sb("seg_inv", [K * H, SLOTS])
        alphaT = sb("alphaT", [K * H, SLOTS])
        msg_b = sb("msg_b", [SLOTS, K * D])
        att_b = sb("att_b", [D, UNROLL, BN])

        a_x = [sem(f"a_x{s}") for s in range(UNROLL)]
        a_dl = [sem(f"a_dl{s}") for s in range(2)]
        a_mask = [sem(f"a_mask{s}") for s in range(UNROLL)]
        a_idx = sem("a_idx")
        a_rows = [sem(f"a_rows{s}") for s in range(UNROLL)]
        a_out = [sem(f"a_out{s}") for s in range(UNROLL)]
        a_hd = sem("a_hd")
        a_hd_ev = sem("a_hd_ev")
        a_slot1h = sem("a_slot1h")
        a_node1h = sem("a_node1h")
        a_u = sem("a_u")
        a_pre = sem("a_pre")
        a_leaky = sem("a_leaky")
        a_prod = sem("a_prod")
        a_score = sem("a_score")
        a_sT = sem("a_sT")
        a_scan = sem("a_scan")
        a_shift = sem("a_shift")
        a_exp = sem("a_exp")
        a_alpha = sem("a_alpha")
        a_alphaT = sem("a_alphaT")
        a_msg = sem("a_msg")
        a_agg = sem("a_agg")
        a_ev = sem("a_ev")
        SCANS = 7

        def att_sync(sp):
            def body(i):
                if i.live():
                    wait(sp, a_hd, i.n(1 - UNROLL))
                    sp.dma_start(xt_b[:, i.slot(4), :], xT[:, bass.ds(i.n(0, BN), BN)]).then_inc(a_x[i.slot(4)], 16)
                    wait(sp, a_slot1h, i.n(-1))
                    sp.dma_start(dl_b[:, i.slot(2), :].unsqueeze(1),
                                 dloc_d[bass.ds(i.n(0, K), K), :].rearrange("k s -> (k s)").partition_broadcast(NB)
                                 ).then_inc(a_dl[i.slot(2)], 16)
                    wait(sp, a_alpha, i.n(1 - UNROLL))
                    sp.dma_start(mask_b[:, i.slot(4), :, :].rearrange("p m s -> p (m s)"),
                                 masks_d[bass.ds(i.n(0, K), K), :, :].rearrange("k m s -> k (m s)").unsqueeze(1)
                                 .broadcast_to([K, H, 4 * SLOTS])).then_inc(a_mask[i.slot(4)], 16)
                k = i.back(2)
                if k.live():
                    sp.wait_ge(a_ev, k.n(1))
                    sp.dma_start(attT[:, bass.ds(k.n(0, BN), BN)], att_b[:, k.slot(4), :]).then_inc(a_out[k.slot(4)], 16)
            walk(sp, body, BATCHES, 2)
            for s in range(UNROLL):
                sp.wait_ge(a_out[s], 16 * len(range(s, BATCHES, UNROLL)))

        def gather(pool, i, table, idx_sem, row_sems, used, base):
            wait(pool, used, i.n(base + 1 - UNROLL) if not i.fixed or i.n() >= UNROLL else 0)
            nc.gpsimd.tensor_copy(idx_b[:, i.slot(4), :], src_c[:, bass.ds(i.n(0, K), K)]).then_inc(idx_sem, 1)
            pool.wait_ge(idx_sem, i.n(base + 1))
            apart(pool)
            for k in range(K):
                nc.gpsimd.indirect_dma_start(
                    rows_b[:, i.slot(4), k, :], None, table,
                    bass.IndirectOffsetOnAxis(ap=idx_b[:, i.slot(4), k:k + 1], axis=0)).then_inc(row_sems[i.slot(4)], 16)

        def att_gpsimd(pool):
            def body(i):
                if i.live():
                    gather(pool, i, hs_table, a_idx, a_rows, a_msg, 0)
            walk(pool, body, BATCHES, 0)

        def att_tensor(pe):
            def body(i):
                k = i.back(1)
                if i.live():
                    pe.wait_ge(a_x[i.slot(4)], i.use(4, 1) * 16)
                    wait(pe, a_hd_ev, i.n())
                    for b in range(K):
                        last = nc.tensor.matmul(wide[0][0:NB, b * D:(b + 1) * D], xt_b[:, i.slot(4), b * NB:(b + 1) * NB],
                                                w_dst_s[:], start=True, stop=True)
                    last.then_inc(a_hd, 1)
                if k.live():
                    pe.wait_ge(a_score, k.n(1))
                    wait(pe, a_shift, k.n())
                    apart(pe)
                    nc.tensor.transpose(bank[0][0:K * H, 0:SLOTS], score_b[:, k.slot(2), :], ident[:]).then_inc(a_sT, 1)
                if i.live():
                    pe.wait_ge(a_hd_ev, i.n(1))
                    pe.wait_ge(a_slot1h, i.n(1))
                    wait(pe, a_pre, i.n())
                    for b in range(K):
                        last = nc.tensor.matmul(wide[1][:, b * D:(b + 1) * D], to_slot[:, i.slot(2), b * SLOTS:(b + 1) * SLOTS],
                                                hd_b[:, i.slot(2), b * D:(b + 1) * D], start=True, stop=True)
                    last.then_inc(a_u, 1)
                if k.live():
                    pe.wait_ge(a_alpha, k.n(1))
                    wait(pe, a_msg, k.n())
                    apart(pe)
                    nc.tensor.transpose(bank[1][:, 0:K * H], alphaT[:], ident[0:K * H, 0:K * H]).then_inc(a_alphaT, 1)
                    pe.wait_ge(a_msg, k.n(1))
                    wait(pe, a_ev, k.n(-1))
                    for b in range(K):
                        last = nc.tensor.matmul(bank[2 + k.slot(2)][:, b * NB:(b + 1) * NB], msg_b[:, b * D:(b + 1) * D],
                                                to_node[:, k.slot(2), b, :], start=True, stop=True)
                    last.then_inc(a_agg, 1)
            walk(pe, body, BATCHES, 1)

        def att_scalar(act):
            def body(i):
                k = i.back(1)
                if i.live():
                    act.wait_ge(a_hd, i.n(1))
                    wait(act, a_u, i.n(-1))
                    nc.scalar.copy(hd_b[:, i.slot(2), :], wide[0][0:NB, 0:BS]).then_inc(a_hd_ev, 1)
                if k.live():
                    act.wait_ge(a_shift, k.n(1))
                    wait(act, a_alpha, k.n())
                    nc.scalar.activation(probs[:], shifted[:], ACT.Exp).then_inc(a_exp, 1)
                if k.live():
                    act.wait_ge(a_agg, k.n(1))
                    wait(act, a_out[k.slot(4)], k.use(4) * 16)
                    nc.scalar.copy(att_b[:, k.slot(4), :], bank[2 + k.slot(2)][:, 0:BN]).then_inc(a_ev, 1)
            walk(act, body, BATCHES, 1)

        def one_hots(dve, i, dl_sems, used_slot, used_node, made_slot, made_node, weighted, base, turns):
            v = nc.vector
            dve.wait_ge(dl_sems[i.slot(2)], (i.use(2, 1) + turns[i.slot(2)]) * 16)
            wait(dve, used_slot, i.n(base - 1))
            v.tensor_scalar(to_slot[:, i.slot(2), :], dl_b[:, i.slot(2), :], iota_col[0:NB, 0:1], None,
                            ALU.is_equal).then_inc(made_slot, 1)
            wait(dve, used_node, i.n(base - 1))
            if weighted:
                for b in range(K):
                    last = v.tensor_scalar(to_node[:, i.slot(2), b, :], iota_row[:, 0:NB], dloc_c[:, bass.ds(i.n(0, K) + b, 1)],
                                           invdeg_c[:, bass.ds(i.n(0, K) + b, 1)], ALU.is_equal, ALU.mult)
                last.then_inc(made_node, 1)
            else:
                v.tensor_tensor(to_node[:, i.slot(2), :, :], iota_row[:, 0:NB].unsqueeze(1).broadcast_to([SLOTS, K, NB]),
                                dloc_c[:, bass.ds(i.n(0, K), K)].unsqueeze(2).broadcast_to([SLOTS, K, NB]),
                                ALU.is_equal).then_inc(made_node, 1)

        def att_vector(dve):
            v = nc.vector

            def body(i):
                k = i.back(1)
                if i.live():
                    one_hots(dve, i, a_dl, a_u, a_agg, a_slot1h, a_node1h, False, 0, [0, 0])
                if k.live():
                    dve.wait_ge(a_sT, k.n(1))
                    dve.wait_ge(a_mask[k.slot(4)], k.use(4, 1) * 16)
                    m = k.slot(4)
                    v.tensor_copy(sT[:], bank[0][0:K * H, 0:SLOTS]).then_inc(a_scan, 1)
                    dve.wait_ge(a_scan, k.n(0, SCANS) + 1)
                    v.tensor_tensor_scan(run_max[:], mask_b[:, m, 0, :], sT[:], -BIG, ALU.add, ALU.max).then_inc(a_scan, 1)
                    dve.wait_ge(a_scan, k.n(0, SCANS) + 2)
                    v.tensor_tensor_scan(seg_max[:, ::-1], mask_b[:, m, 1, ::-1], run_max[:, ::-1], -BIG, ALU.add, ALU.max).then_inc(a_scan, 1)
                    dve.wait_ge(a_scan, k.n(0, SCANS) + 3)
                    wait(dve, a_exp, k.n())
                    v.tensor_tensor(shifted[:], sT[:], seg_max[:], ALU.subtract).then_inc(a_shift, 1)
                if i.live():
                    dve.wait_ge(a_u, i.n(1))
                    dve.wait_ge(a_rows[i.slot(4)], i.use(4, 1) * 16 * K)
                    wait(dve, a_leaky, i.n(-1))
                    v.tensor_tensor(pre_b[:, i.slot(2), :], wide[1][:, 0:K * D], rows_b[:, i.slot(4), :, :].rearrange("p k d -> p (k d)"),
                                    ALU.add).then_inc(a_pre, 1)
                    dve.wait_ge(a_pre, i.n(1))
                    wait(dve, a_prod, i.n(-1))
                    v.scalar_tensor_tensor(leaky_b[:, i.slot(2), :], pre_b[:, i.slot(2), :], 0.2, pre_b[:, i.slot(2), :],
                                           ALU.mult, ALU.max).then_inc(a_leaky, 1)
                if k.live():
                    dve.wait_ge(a_exp, k.n(1))
                    v.tensor_tensor_scan(run_sum[:], mask_b[:, m, 2, :], probs[:], 0.0, ALU.mult, ALU.add).then_inc(a_scan, 1)
                    dve.wait_ge(a_scan, k.n(0, SCANS) + 4)
                    v.tensor_tensor_scan(seg_sum[:, ::-1], mask_b[:, m, 3, ::-1], run_sum[:, ::-1], 0.0, ALU.mult, ALU.max).then_inc(a_scan, 1)
                    dve.wait_ge(a_scan, k.n(0, SCANS) + 5)
                    v.tensor_scalar(seg_eps[:], seg_sum[:], 1e-8, None, ALU.add).then_inc(a_scan, 1)
                    dve.wait_ge(a_scan, k.n(0, SCANS) + 6)
                    v.reciprocal(seg_inv[:], seg_eps[:]).then_inc(a_scan, 1)
                    dve.wait_ge(a_scan, k.n(0, SCANS) + 7)
                    wait(dve, a_alphaT, k.n())
                    v.tensor_tensor(alphaT[:], probs[:], seg_inv[:], ALU.mult).then_inc(a_alpha, 1)
                if i.live():
                    dve.wait_ge(a_leaky, i.n(1))
                    wait(dve, a_score, i.n())
                    v.tensor_tensor(prod_b[:].rearrange("p (k d) -> p k d", k=K), leaky_b[:, i.slot(2), :].rearrange("p (k d) -> p k d", k=K),
                                    attn_bc[:].unsqueeze(1).broadcast_to([SLOTS, K, D]), ALU.mult).then_inc(a_prod, 1)
                if k.live():
                    dve.wait_ge(a_alphaT, k.n(1))
                    wait(dve, a_agg, k.n())
                    v.tensor_tensor(msg_b[:].rearrange("p (h d) -> p h d", d=HD),
                                    rows_b[:, k.slot(4), :, :].rearrange("p k (h d) -> p (k h) d", d=HD),
                                    bank[1][:, 0:K * H].unsqueeze(2).broadcast_to([SLOTS, K * H, HD]), ALU.mult).then_inc(a_msg, 1)
                if i.live():
                    dve.wait_ge(a_prod, i.n(1))
                    wait(dve, a_sT, i.n(-1))
                    v.tensor_reduce(score_b[:, i.slot(2), :], prod_b[:].rearrange("p (h d) -> p h d", d=HD),
                                    AXIS.X, ALU.add).then_inc(a_score, 1)
            walk(dve, body, BATCHES, 1)

        own_space()
        at_in = sb("at_in", [D, 2, TN])
        xr_in = sb("xr_in", [TP, 2, TT, D])
        xbeta = sb("xbeta", [TP, TT, D])
        xbout = sb("xbout", [TP, TT, D])
        res_n = sb("res_n", [TP, TT, D])
        stats = sb("stats", [TP, TT, 6])
        mean_var = sb("mean_var", [TP, 2, TT, 2])
        logv = sb("logv", [TP, 2, TT])
        rstd = sb("rstd", [TP, 2, TT])
        shift_n = sb("shift_n", [TP, 2, TT])
        norm1 = sb("norm1", [TP, TT, D])
        scaled = sb("scaled", [TP, TT, D])
        sum_n = sb("sum_n", [TP, TT, D])
        x1_n = sb("x1_n", [TP, 2, TT, D])
        resid_n = sb("resid_n", [TP, 2, TT, D])
        x1T_n = sb("x1T_n", [D, 2, TN])
        y_n = sb("y_n", [TP, 2, TT, D])
        n_at = [sem(f"n_at{s}") for s in range(2)]
        n_x = [sem(f"n_xin{s}") for s in range(2)]
        n_x1o = [sem(f"n_x1o{s}") for s in range(2)]
        n_x1To = [sem(f"n_x1To{s}") for s in range(2)]
        n_yo = [sem(f"n_yo{s}") for s in range(2)]
        n_rd, n_o, n_xb, n_xo, n_res, n_st, n_mv, n_log, n_rstd, n_sh, n_norm, n_scaled, n_sum, n_x1, n_T, n_Tev, n_y, n_yev = [
            sem("n_" + s) for s in ("rd", "o", "xb", "xo", "res", "st", "mv", "log", "rstd", "sh", "norm", "scaled", "sum", "x1", "T", "Tev", "y", "yev")]

        def norm_sync(sp):
            def body(i):
                if i.live():
                    wait(sp, n_o, i.n(-1))
                    sp.dma_start(at_in[:, i.slot(2), :], attT[:, bass.ds(i.n(0, TN), TN)]).then_inc(n_at[i.slot(2)], 16)
                    wait(sp, n_xb, i.n(-1))
                    sp.dma_start(xr_in[:, i.slot(2), :, :], rows_of(x, i)).then_inc(n_x[i.slot(2)], 16)
                k = i.back(1)
                if k.live():
                    sp.wait_ge(n_rd, k.n(1))
                    sp.dma_start(rows_of(resid_rows, k), resid_n[:, k.slot(2), :, :]).then_inc(n_x1o[k.slot(2)], 16)
                    sp.wait_ge(n_Tev, k.n(1))
                    apart(sp)
                    sp.dma_start(xT_l[0][:, bass.ds(k.n(0, TN), TN)], x1T_n[:, k.slot(2), :]).then_inc(n_x1To[k.slot(2)], 16)
                    sp.wait_ge(n_yev, k.n(1))
                    sp.dma_start(rows_of(y_table[0], k), y_n[:, k.slot(2), :, :]).then_inc(n_yo[k.slot(2)], 16)
            walk(sp, body, TILES, 1)
            for s in range(2):
                for o in (n_x1o, n_x1To, n_yo):
                    sp.wait_ge(o[s], 16 * len(range(s, TILES, 2)))

        def norm_gpsimd(pool):
            def body(i):
                if i.live():
                    pool.wait_ge(n_x[i.slot(2)], i.use(2, 1) * 16)
                    wait(pool, n_res, i.n())
                    nc.gpsimd.tensor_tensor(xbout[:], xr_in[:, i.slot(2), :, :], bout_bc[0:TP, :].unsqueeze(1).broadcast_to([TP, TT, D]), ALU.add).then_inc(n_xo, 1)
                    wait(pool, n_sum, i.n())
                    nc.gpsimd.tensor_tensor(xbeta[:], xr_in[:, i.slot(2), :, :], beta_bc[0:TP, :].unsqueeze(1).broadcast_to([TP, TT, D]), ALU.add).then_inc(n_xb, 1)
                    pool.wait_ge(n_norm, i.n(1))
                    nc.gpsimd.tensor_tensor(scaled[:], norm1[:], gamma_bc[0:TP, :].unsqueeze(1).broadcast_to([TP, TT, D]), ALU.mult).then_inc(n_scaled, 1)
                k = i.back(1)
                if k.live():
                    pool.wait_ge(n_x1, k.n(1))
                    wait(pool, n_x1o[k.slot(2)], k.use(2) * 16)
                    nc.gpsimd.tensor_tensor(resid_n[:, k.slot(2), :, :], x1_n[:, k.slot(2), :, :], dpb_bc[0:TP, :].unsqueeze(1).broadcast_to([TP, TT, D]), ALU.add).then_inc(n_rd, 1)
            walk(pool, body, TILES, 1)

        def norm_tensor(pe):
            def body(i):
                if i.live():
                    pe.wait_ge(n_at[i.slot(2)], i.use(2, 1) * 16)
                    wait(pe, n_res, i.n())
                    for t in range(TT):
                        last = nc.tensor.matmul(bank[0][0:TP, t * D:(t + 1) * D], at_in[:, i.slot(2), t * TP:(t + 1) * TP],
                                                w_out_s[:], start=True, stop=True)
                    last.then_inc(n_o, 1)
                k = i.back(1)
                if k.live():
                    pe.wait_ge(n_x1, k.n(1))
                    wait(pe, n_Tev, k.n())
                    apart(pe)
                    for t in range(TT):
                        last = nc.tensor.transpose(bank[1][:, t * TP:(t + 1) * TP], x1_n[:, k.slot(2), t, :], ident[0:TP, 0:TP])
                    last.then_inc(n_T, 1)
                    pe.wait_ge(n_Tev, k.n(1))
                    wait(pe, n_yev, k.n())
                    for t in range(TT):
                        last = nc.tensor.matmul(bank[2][0:TP, t * D:(t + 1) * D], x1T_n[:, k.slot(2), t * TP:(t + 1) * TP],
                                                psi_src_s[:, 0, :], start=True, stop=True)
                    last.then_inc(n_y, 1)
            walk(pe, body, TILES, 1)

        def norm_stats(dve, i, source, which, mv_sem, st_sem, sh_sem, rstd_sem, base, per, rows, tiles, st, mv, sh, rs):
            v = nc.vector
            for t in range(tiles):
                last = v.bn_stats(st[:, t, :], source(t))
            last.then_inc(st_sem, 1)
            dve.wait_ge(st_sem, i.n(0, per) + which + 1 + base)
            apart(dve)
            for t in range(tiles):
                last = v.bn_aggr(mv[:, which, t, :], st[:, t, :])
            last.then_inc(mv_sem, 1)
            dve.wait_ge(rstd_sem, i.n(0, per) + which + 1 + base)
            v.scalar_tensor_tensor(sh[:, which, :], mv[:, which, :, 0], -1.0, rs[:, which, :], ALU.mult, ALU.mult).then_inc(sh_sem, 1)

        def norm_vector(dve):
            v = nc.vector

            def body(i):
                if i.live():
                    dve.wait_ge(n_o, i.n(1))
                    dve.wait_ge(n_xo, i.n(1))
                    v.tensor_tensor(flat(res_n[:]), bank[0][0:TP, :], flat(xbout[:]), ALU.add).then_inc(n_res, 1)
                    dve.wait_ge(n_res, i.n(1))
                    norm_stats(dve, i, lambda t: res_n[:, t, :], 0, n_mv, n_st, n_sh, n_rstd, 0, 2, TP, TT, stats, mean_var, shift_n, rstd)
                    dve.wait_ge(n_scaled, i.n(1))
                    dve.wait_ge(n_xb, i.n(1))
                    wait(dve, n_x1, i.n())
                    v.tensor_tensor(sum_n[:], scaled[:], xbeta[:], ALU.add).then_inc(n_sum, 1)
                    dve.wait_ge(n_sum, i.n(1))
                    norm_stats(dve, i, lambda t: sum_n[:, t, :], 1, n_mv, n_st, n_sh, n_rstd, 0, 2, TP, TT, stats, mean_var, shift_n, rstd)
            walk(dve, body, TILES, 0)

        def inv_std(act, i, which, mv, lg, rs, mv_sem, log_sem, rstd_sem, base, per):
            act.wait_ge(mv_sem, i.n(0, per) + which + 1 + base)
            p = mv.shape[0]
            nc.scalar.activation(lg[:, which, :], mv[:, which, :, 1], ACT.Ln, bias=eps_col[0:p, 0:1]).then_inc(log_sem, 1)
            act.wait_ge(log_sem, i.n(0, per) + which + 1 + base)
            nc.scalar.activation(rs[:, which, :], lg[:, which, :], ACT.Exp, scale=-0.5).then_inc(rstd_sem, 1)

        def norm_scalar(act):
            def body(i):
                if i.live():
                    inv_std(act, i, 0, mean_var, logv, rstd, n_mv, n_log, n_rstd, 0, 2)
                    act.wait_ge(n_sh, i.n(0, 2) + 1)
                    wait(act, n_scaled, i.n())
                    for t in range(TT):
                        last = nc.scalar.activation(norm1[:, t, :], res_n[:, t, :], ACT.Identity, bias=shift_n[:, 0, t:t + 1], scale=rstd[:, 0, t:t + 1])
                    last.then_inc(n_norm, 1)
                k = i.back(1)
                if k.live():
                    act.wait_ge(n_T, k.n(1))
                    wait(act, n_x1To[k.slot(2)], k.use(2) * 16)
                    nc.scalar.copy(x1T_n[:, k.slot(2), :], bank[1][:, 0:TN]).then_inc(n_Tev, 1)
                if i.live():
                    inv_std(act, i, 1, mean_var, logv, rstd, n_mv, n_log, n_rstd, 0, 2)
                    act.wait_ge(n_sh, i.n(0, 2) + 2)
                    wait(act, n_rd, i.n(-1))
                    wait(act, n_T, i.n(-1))
                    for t in range(TT):
                        last = nc.scalar.activation(x1_n[:, i.slot(2), t, :], sum_n[:, t, :], ACT.Identity, bias=shift_n[:, 1, t:t + 1], scale=rstd[:, 1, t:t + 1])
                    last.then_inc(n_x1, 1)
                if k.live():
                    act.wait_ge(n_y, k.n(1))
                    wait(act, n_yo[k.slot(2)], k.use(2) * 16)
                    nc.scalar.copy(flat(y_n[:, k.slot(2), :, :]), bank[2][0:TP, :]).then_inc(n_yev, 1)
            walk(act, body, TILES, 1)

        give_back()
        z_b = hd_b
        m_b = leaky_b
        agg_b = sb("agg_b", [D, 2, BN])
        relu_b = sb("relu_b", [D, BN])
        xnew_b = sb("xnew_b", [D, UNROLL, BN])
        yrow_b = sb("yrow_b", [NB, UNROLL, K, D])
        x1_b = sb("x1_b", [NB, 2, K, D])
        fstats = sb("fstats", [NB, K, 6])
        fmv = sb("fmv", [NB, 1, K, 2])
        flog = sb("flog", [NB, 1, K])
        frstd = sb("frstd", [NB, 1, K])
        fshift = sb("fshift", [NB, 1, K])
        fsum = sb("fsum", [NB, K, D])
        def uses(slots, l):
            return [l * len(range(s, BATCHES, slots)) for s in range(slots)]

        def block_rows(table, i):
            return table[bass.ds(i.n(0, BN), BN), :].rearrange("(b p) d -> p b d", p=NB)

        def layer_sync(sp, l):
            base, u4, u2 = l * BATCHES, uses(4, l), uses(2, l)
            last_layer = l == LAYERS - 1

            def body(i):
                if i.live():
                    if not i.fixed or i.n() >= UNROLL:
                        sp.wait_ge(g_xnew, i.n(base + 1 - UNROLL))
                    sp.dma_start(xt_b[:, i.slot(4), :], xT_l[l][:, bass.ds(i.n(0, BN), BN)]).then_inc(g_x[i.slot(4)], 16)
                    wait(sp, g_slot1h, i.n(base - 1))
                    sp.dma_start(dl_b[:, i.slot(2), :].unsqueeze(1),
                                 dloc_d[bass.ds(i.n(0, K), K), :].rearrange("k s -> (k s)").partition_broadcast(NB)
                                 ).then_inc(g_dl[i.slot(2)], 16)
                    if last_layer:
                        wait(sp, f_sum, i.n(-1))
                        sp.dma_start(x1_b[:, i.slot(2), :, :], block_rows(resid_rows, i)).then_inc(g_x1[i.slot(2)], 16)
                k = i.back(2)
                if k.live():
                    if not last_layer:
                        sp.wait_ge(g_xnew, k.n(base + 1))
                        sp.dma_start(xT_l[l + 1][:, bass.ds(k.n(0, BN), BN)], xnew_b[:, k.slot(4), :]).then_inc(g_xo[k.slot(4)], 16)
                    sp.wait_ge(g_yev, k.n(base + 1))
                    sp.dma_start(block_rows(out if last_layer else y_table[l + 1], k), yrow_b[:, k.slot(4), :, :]).then_inc(g_yo[k.slot(4)], 16)
            walk(sp, body, BATCHES, 2)
            for s in range(UNROLL):
                sp.wait_ge(g_yo[s], 16 * uses(4, l + 1)[s])
                sp.wait_ge(g_xo[s], 16 * uses(4, min(l + 1, LAYERS - 1))[s])

        def layer_gpsimd(pool, l):
            def body(i):
                if i.live():
                    gather(pool, i, y_table[l], g_idx, g_rows, g_pre, l * BATCHES)
            walk(pool, body, BATCHES, 0)

        def layer_tensor(pe, l):
            base, u4 = l * BATCHES, uses(4, l)
            last_w = dp_s[:] if l == LAYERS - 1 else psi_src_s[:, min(l + 1, LAYERS - 1), :]

            def body(i):
                k, y = i.back(1), i.back(2)
                if i.live():
                    pe.wait_ge(g_x[i.slot(4)], (i.use(4, 1) + u4[i.slot(4)]) * 16)
                    wait(pe, g_zev, i.n(base))
                    for b in range(K):
                        last = nc.tensor.matmul(wide[0][0:NB, b * D:(b + 1) * D], xt_b[:, i.slot(4), b * NB:(b + 1) * NB],
                                                psi_dst_s[:, l, :], start=True, stop=True)
                    last.then_inc(g_z, 1)
                if k.live():
                    pe.wait_ge(g_m, k.n(base + 1))
                    pe.wait_ge(g_node1h, k.n(base + 1))
                    wait(pe, g_aggev, k.n(base))
                    for b in range(K):
                        last = nc.tensor.matmul(bank[0][:, b * NB:(b + 1) * NB], m_b[:, k.slot(2), b * D:(b + 1) * D],
                                                to_node[:, k.slot(2), b, :], start=True, stop=True)
                    last.then_inc(g_agg, 1)
                if y.live():
                    pe.wait_ge(g_xnew, y.n(base + 1))
                    wait(pe, g_yev, y.n(base))
                    for b in range(K):
                        where = bank[2][0:NB, b * D:(b + 1) * D] if b < 4 else bank[3][0:NB, 0:D]
                        last = nc.tensor.matmul(where, xnew_b[:, y.slot(4), b * NB:(b + 1) * NB], last_w, start=True, stop=True)
                    last.then_inc(g_y, 1)
                if i.live():
                    pe.wait_ge(g_zev, i.n(base + 1))
                    pe.wait_ge(g_slot1h, i.n(base + 1))
                    wait(pe, g_pre, i.n(base))
                    for b in range(K):
                        last = nc.tensor.matmul(wide[1][:, b * D:(b + 1) * D], to_slot[:, i.slot(2), b * SLOTS:(b + 1) * SLOTS],
                                                z_b[:, i.slot(2), b * D:(b + 1) * D], start=True, stop=True)
                    last.then_inc(g_u, 1)
                if k.live():
                    wait(pe, g_relu, k.n(base))
                    nc.tensor.matmul(bank[1][:, 0:BN], phi_x_s[:, l, :], xt_b[:, k.slot(4), :], start=True, stop=False)
                    pe.wait_ge(g_aggev, k.n(base + 1))
                    nc.tensor.matmul(bank[1][:, 0:BN], phi_agg_s[:, l, :], agg_b[:, k.slot(2), :], start=False, stop=True).then_inc(g_q, 1)
            walk(pe, body, BATCHES, 2)

        def layer_scalar(act, l):
            base, u4 = l * BATCHES, uses(4, l)
            last_layer = l == LAYERS - 1

            def body(i):
                k, y = i.back(1), i.back(2)
                if k.live():
                    act.wait_ge(g_agg, k.n(base + 1))
                    wait(act, g_q, k.n(base - 1))
                    nc.scalar.copy(agg_b[:, k.slot(2), :], bank[0][:, 0:BN]).then_inc(g_aggev, 1)
                if y.live() and not last_layer:
                    act.wait_ge(g_y, y.n(base + 1))
                    wait(act, g_yo[y.slot(4)], (y.use(4) + u4[y.slot(4)]) * 16)
                    nc.scalar.copy(yrow_b[:, y.slot(4), 0:4, :].rearrange("p b d -> p (b d)"), bank[2][0:NB, :])
                    nc.scalar.copy(yrow_b[:, y.slot(4), 4, :], bank[3][0:NB, 0:D]).then_inc(g_yev, 1)
                if y.live() and last_layer:
                    inv_std(act, y, 0, fmv, flog, frstd, f_mv, f_log, f_rstd, 0, 1)
                    act.wait_ge(f_sh, y.n(1))
                    wait(act, g_yo[y.slot(4)], (y.use(4) + u4[y.slot(4)]) * 16)
                    for b in range(K):
                        last = nc.scalar.activation(yrow_b[:, y.slot(4), b, :], fsum[:, b, :], ACT.Identity,
                                                    bias=fshift[:, 0, b:b + 1], scale=frstd[:, 0, b:b + 1])
                    last.then_inc(g_yev, 1)
                if k.live():
                    act.wait_ge(g_q, k.n(base + 1))
                    wait(act, g_xnew, k.n(base))
                    nc.scalar.activation(relu_b[:], bank[1][:, 0:BN], ACT.Relu, bias=phi_b_col[:, l:l + 1]).then_inc(g_relu, 1)
                if i.live():
                    act.wait_ge(g_pre, i.n(base + 1))
                    wait(act, g_agg, i.n(base - 1))
                    nc.scalar.activation(m_b[:, i.slot(2), :], pre_b[:, i.slot(2), :], ACT.Relu).then_inc(g_m, 1)
            walk(act, body, BATCHES, 2)

        def layer_vector(dve, l):
            base, u4, u2 = l * BATCHES, uses(4, l), uses(2, l)
            last_layer = l == LAYERS - 1
            v = nc.vector

            def body(i):
                k, y = i.back(1), i.back(2)
                if i.live():
                    one_hots(dve, i, g_dl, g_u, g_agg, g_slot1h, g_node1h, True, base, u2)
                    dve.wait_ge(g_z, i.n(base + 1))
                    v.tensor_tensor(z_b[:, i.slot(2), :].rearrange("p (k d) -> p k d", k=K), wide[0][0:NB, 0:BS].rearrange("p (k d) -> p k d", k=K),
                                    psi_b_bc[0:NB, l, :].unsqueeze(1).broadcast_to([NB, K, D]), ALU.add).then_inc(g_zev, 1)
                if y.live() and last_layer:
                    dve.wait_ge(g_y, y.n(base + 1))
                    dve.wait_ge(g_x1[y.slot(2)], y.use(2, 1) * 16)
                    wait(dve, g_yev, y.n(base))
                    v.tensor_tensor(fsum[:, 0:4, :], bank[2][0:NB, :].rearrange("p (b d) -> p b d", d=D), x1_b[:, y.slot(2), 0:4, :], ALU.add)
                    v.tensor_tensor(fsum[:, 4, :], bank[3][0:NB, 0:D], x1_b[:, y.slot(2), 4, :], ALU.add).then_inc(f_sum, 1)
                if i.live():
                    dve.wait_ge(g_u, i.n(base + 1))
                    dve.wait_ge(g_rows[i.slot(4)], (i.use(4, 1) + u4[i.slot(4)]) * 16 * K)
                    wait(dve, g_m, i.n(base - 1))
                    v.tensor_tensor(pre_b[:, i.slot(2), :], wide[1][:, 0:K * D], rows_b[:, i.slot(4), :, :].rearrange("p k d -> p (k d)"),
                                    ALU.add).then_inc(g_pre, 1)
                if y.live() and last_layer:
                    dve.wait_ge(f_sum, y.n(1))
                    norm_stats(dve, y, lambda t: fsum[:, t, :], 0, f_mv, f_st, f_sh, f_rstd, 0, 1, NB, K, fstats, fmv, fshift, frstd)
                if k.live():
                    dve.wait_ge(g_relu, k.n(base + 1))
                    if not last_layer:
                        wait(dve, g_xo[k.slot(4)], (k.use(4) + u4[k.slot(4)]) * 16)
                    if not k.fixed or k.n() >= UNROLL or base:
                        wait(dve, g_y, k.n(base + 1 - UNROLL))
                    v.tensor_tensor(xnew_b[:, k.slot(4), :], relu_b[:], xt_b[:, k.slot(4), :], ALU.add).then_inc(g_xnew, 1)
            walk(dve, body, BATCHES, 2)

        with nc.Block() as block:
            @block.sync
            def _(sp):
                prep_sync(sp)
                sp.sem_inc(phase_done, 1)
                table_sync(sp)
                sp.sem_inc(phase_done, 1)

                def slow():
                    zero_sync(sp)
                    general(sp, node_sync, edge_sync, 0, len(ATTEND))
                by_path(sp, lambda: att_sync(sp), slow)
                sp.sem_inc(phase_done, 1)
                norm_sync(sp)
                sp.sem_inc(phase_done, 1)

                def fast_layers():
                    for l in range(LAYERS):
                        layer_sync(sp, l)
                        sp.sem_inc(phase_done, 1)
                by_path(sp, fast_layers, lambda: general(sp, node_sync, edge_sync, len(ATTEND), len(PLAN)))

            @block.gpsimd
            def _(pool):
                prep_gpsimd(pool)
                begin(pool, 2)
                by_path(pool, lambda: att_gpsimd(pool), lambda: general(pool, None, edge_gpsimd, 0, len(ATTEND)))
                begin(pool, 3)
                norm_gpsimd(pool)

                def fast_layers():
                    for l in range(LAYERS):
                        begin(pool, 4 + l)
                        layer_gpsimd(pool, l)
                by_path(pool, fast_layers, lambda: general(pool, None, edge_gpsimd, len(ATTEND), len(PLAN)))

            @block.tensor
            def _(pe):
                prep_tensor(pe)
                begin(pe, 1)
                table_tensor(pe)
                begin(pe, 2)
                by_path(pe, lambda: att_tensor(pe), lambda: general(pe, node_tensor, edge_tensor, 0, len(ATTEND)))
                begin(pe, 3)
                norm_tensor(pe)

                def fast_layers():
                    for l in range(LAYERS):
                        begin(pe, 4 + l)
                        layer_tensor(pe, l)
                by_path(pe, fast_layers, lambda: general(pe, node_tensor, edge_tensor, len(ATTEND), len(PLAN)))

            @block.scalar
            def _(act):
                nc.scalar.preload_act_table_set("natural_log_exp_and_others")
                begin(act, 1)
                table_scalar(act)
                begin(act, 2)
                by_path(act, lambda: att_scalar(act), lambda: general(act, node_scalar, edge_scalar, 0, len(ATTEND)))
                begin(act, 3)
                norm_scalar(act)

                def fast_layers():
                    for l in range(LAYERS):
                        begin(act, 4 + l)
                        layer_scalar(act, l)
                by_path(act, fast_layers, lambda: general(act, node_scalar, edge_scalar, len(ATTEND), len(PLAN)))

            @block.vector
            def _(dve):
                prep_vector(dve)
                begin(dve, 2)

                def slow():
                    zero_vector(dve)
                    general(dve, node_vector, edge_vector, 0, len(ATTEND))
                by_path(dve, lambda: att_vector(dve), slow)
                begin(dve, 3)
                norm_vector(dve)

                def fast_layers():
                    for l in range(LAYERS):
                        begin(dve, 4 + l)
                        layer_vector(dve, l)
                by_path(dve, fast_layers, lambda: general(dve, node_vector, edge_vector, len(ATTEND), len(PLAN)))


def kernel(**inputs):
    import numpy as np
    import concourse.bacc as bacc
    from concourse.bass_utils import run_bass_kernel_spmd

    a = {name: np.asarray(value) for name, value in inputs.items()}
    src = np.zeros([EROWS * SLOTS], np.int32)
    dst = np.full([EROWS * SLOTS], 1 << 20, np.int32)
    src[:E] = a["src"]
    dst[:E] = a["dst"]
    psi, phi = a["L1_gnn_psi_w"], a["L1_gnn_phi_w"]
    arrays = {
        "xT": a["x"].T, "x": a["x"],
        "src_dst": np.stack([src.reshape(EROWS, SLOTS), dst.reshape(EROWS, SLOTS)], axis=1).reshape(EROWS, 2 * SLOTS),
        "dst_cols": a["dst"].reshape(GP, EC), "src_flat": a["src"].reshape(E, 1),
        "dst_pad": np.concatenate([np.full(1, -1, np.int32), a["dst"], np.full(1, -1, np.int32)]).reshape(E + 2, 1),
        "w_src": a["L0_gnn_W_src"], "w_dst": a["L0_gnn_W_dst"], "attn": a["L0_gnn_attn"].reshape(1, D),
        "w_out": a["L0_gnn_W_out"], "b_out": a["L0_gnn_b_out"].reshape(1, D),
        "gamma": a["L0_gnn_gamma"].reshape(1, D), "beta": a["L0_gnn_beta"].reshape(1, D),
        "psi_dst": psi[:, :D, :], "psi_src": psi[:, D:, :], "psi_b": a["L1_gnn_psi_b"],
        "phi_x": phi[:, :D, :], "phi_agg": phi[:, D:, :], "phi_b": a["L1_gnn_phi_b"].T,
        "dp_w": a["L1_gnn_dp_w"], "dp_b": a["L1_gnn_dp_b"].reshape(1, D),
    }
    nc = bacc.Bacc("TRN2", target_bir_lowering=False, num_devices=1)
    given, args = {}, []
    for name, value in arrays.items():
        value = np.ascontiguousarray(value)
        given["in_" + name] = value
        args.append(nc.dram_tensor("in_" + name, value.shape, mybir.dt.from_np(value.dtype), kind="ExternalInput").ap())
    args.append(nc.dram_tensor("out_x", [N, D], FP32, kind="ExternalOutput").ap())
    gnn_kernel(nc, *args)
    return run_bass_kernel_spmd(nc, [given], core_ids=[0]).results[0]["out_x"]
```

```python
import concourse.bass as bass
from concourse import mybir
from contextlib import ExitStack

FP32 = mybir.dt.float32
I32 = mybir.dt.int32
ALU = mybir.AluOpType
ACT = mybir.ActivationFunctionType
AXIS = mybir.AxisListType

N = 50000
E = 50000
D = 128
H = 8
HD = D // H
NB = 80
SLOTS = 128
NBLK = N // NB
K = 5
BATCHES = NBLK // K
BN = K * NB
CT = 4
CP = BN // CT
BS = K * SLOTS
UNROLL = 6
TP, TT = 125, 4
TN = TP * TT
TILES = N // TN
LAYERS = 3
EPS = 1e-5
BIG = 1e30
GP = 125
GG = NBLK // GP
EROWS = 392
QN = 25
EC = E // GP


class At:

    def __init__(self, turn, off, count):
        self.turn, self.off, self.count = turn, off, count
        self.fixed = isinstance(turn, int)

    def back(self, lag):
        return At(self.turn, self.off - lag, self.count)

    def live(self):
        return not self.fixed or 0 <= UNROLL * self.turn + self.off < self.count

    def n(self, plus=0, times=1):
        return self.turn * (UNROLL * times) + (self.off + plus) * times

    def slot(self, slots):
        return self.off % slots

    def use(self, slots, plus=0):
        return self.turn * (UNROLL // slots) + self.off // slots + plus


def walk(eng, body, count, lag, reach=2, pause=None, meanwhile=None):
    first = -(-(lag + reach) // UNROLL)
    for off in range(first * UNROLL):
        body(At(0, off, count))
    turns = count // UNROLL
    for start, end in ((first, turns),) if pause is None else ((first, pause), (pause, turns)):
        if start == pause:
            meanwhile()
        with eng.Fori(start, end) as turn:
            for off in range(UNROLL):
                body(At(turn, off, count))
    for off in range(count % UNROLL + lag):
        body(At(0, turns * UNROLL + off, count))


def wait(eng, sem, value):
    if not isinstance(value, int) or value > 0:
        eng.wait_ge(sem, value)


def gnn_kernel(nc, xT, x, src_dst, dst_cols, src_flat, dst_pad, w_src, w_dst, attn, w_out, b_out, gamma, beta,
               psi_dst, psi_src, psi_b, phi_x, phi_agg, phi_b, dp_w, dp_b, out):
    ctx = ExitStack()
    with ctx:
        scope = [ctx]

        def sb(name, shape, dt=FP32):
            return scope[-1].enter_context(nc.sbuf_tensor(name, shape, dt))

        def own_space():
            scope.append(ExitStack())

        def give_back():
            scope.pop().close()

        def sem(name):
            return ctx.enter_context(nc.semaphore(name))

        def dram(name, shape, dt=FP32):
            return nc.dram_tensor(name, shape, dt, kind="Internal").ap()

        hs_table = dram("hs_table", [N, D])
        attT = dram("attT", [D, N])
        resid_rows = dram("resid_rows", [N, D])
        xT_l = [dram(f"xT_{l}", [D, N]) for l in range(LAYERS)]
        y_table = [dram(f"y_table_{l}", [N, D]) for l in range(LAYERS)]
        masks_d = dram("masks_d", [NBLK, 4, SLOTS])
        dloc_d = dram("dloc_d", [NBLK, SLOTS])
        start_d = dram("start_d", [QN, QN])

        ident = sb("ident", [128, 128])
        iota_row = sb("iota_row", [128, 128])
        iota_col = sb("iota_col", [128, 1])
        eps_col = sb("eps_col", [128, 1])
        tiny_col = sb("tiny_col", [128, 1])
        one_col = sb("one_col", [128, 1])
        iota_i = sb("iota_i", [128, 128], I32)
        iota_ci = sb("iota_ci", [128, 1], I32)
        w_src_s = sb("w_src_s", [D, D])
        w_dst_s = sb("w_dst_s", [D, D])
        w_out_s = sb("w_out_s", [D, D])
        dp_s = sb("dp_s", [D, D])
        psi_dst_s = sb("psi_dst_s", [D, LAYERS, D])
        psi_src_s = sb("psi_src_s", [D, LAYERS, D])
        phi_x_s = sb("phi_x_s", [D, LAYERS, D])
        phi_agg_s = sb("phi_agg_s", [D, LAYERS, D])
        psi_b_bc = sb("psi_b_bc", [128, LAYERS, D])
        phi_b_col = sb("phi_b_col", [D, LAYERS])
        attn_bc = sb("attn_bc", [128, D])
        gamma_bc = sb("gamma_bc", [128, D])
        beta_bc = sb("beta_bc", [128, D])
        bout_bc = sb("bout_bc", [128, D])
        dpb_bc = sb("dpb_bc", [128, D])

        dloc_c = sb("dloc_c", [SLOTS, NBLK])
        invdeg_c = sb("invdeg_c", [SLOTS, NBLK])
        src_c = sb("src_c", [SLOTS, NBLK], I32)

        fits_i = sb("fits_i", [1, 1], I32)

        bank = [ctx.enter_context(nc.psum_tensor(f"bank{i}", [128, 512], FP32)) for i in range(4)]
        wide = [ctx.enter_context(nc.psum_tensor(f"wide{i}", [128, 1024], FP32)) for i in range(2)]

        phase_done = sem("phase_done")
        const_in = sem("const_in")
        iota_made = sem("iota_made")
        const_made = sem("const_made")
        ALL_CONSTS = 16 * (4 + 4 * LAYERS + LAYERS + 1 + 5)

        waits_apart = sem("waits_apart")

        def apart(eng):
            eng.sem_inc(waits_apart, 1)

        def flat(ap):
            return ap.rearrange("p t d -> p (t d)")

        def begin(eng, phases):
            if phases:
                eng.wait_ge(phase_done, phases)

        own_space()
        dst_i = sb("dst_i", [GP, EC], I32)
        dst_f = sb("dst_f", [GP, EC])
        quot = sb("quot", [GP, EC])
        resid = sb("resid", [GP, EC])
        is_q = sb("is_q", [GP, EC, QN], mybir.dt.bfloat16)
        is_below = sb("is_below", [GP, EC, QN + 1], mybir.dt.bfloat16)
        counts = sb("counts", [QN, QN + 1])
        upper = sb("upper", [QN, QN])
        start_q = sb("start_q", [QN, QN])
        filled = sb("filled", [QN, QN])
        fullest = sb("fullest", [QN, 1])
        fullest_row = sb("fullest_row", [1, 1])
        fits_f = sb("fits_f", [1, 1])
        start_s = sb("start_s", [GP, GG])
        start_i = sb("start_i", [GP, GG], I32)
        row_i = sb("row_i", [GP, 2, GG], I32)
        rot_i = sb("rot_i", [GP, GG], I32)
        bit_i = sb("bit_i", [GP, 7, GG], I32)
        bit_f = sb("bit_f", [GP, 7, GG, 2])
        win_i = sb("win_i", [GP, GG, 2, 2, SLOTS], I32)
        win = [sb(f"win{i}", [GP, GG, 2, 2 * SLOTS]) for i in range(2)]
        step = sb("step", [GP, GG, 2, 2 * SLOTS])
        base_i = sb("base_i", [GP, GG], I32)
        base_f = sb("base_f", [GP, GG])
        dloc_r = sb("dloc_r", [GP, GG, SLOTS])
        src_r = sb("src_r", [GP, GG, SLOTS])
        masks = sb("masks", [GP, GG, 4, SLOTS])
        ones_r = sb("ones_r", [GP, SLOTS])
        cnt_f = sb("cnt_f", [GP, GG, SLOTS])
        deg_r = sb("deg_r", [GP, GG, SLOTS])
        invdeg_r = sb("invdeg_r", [GP, GG, SLOTS])

        dst_in = sem("dst_in")
        hot_ready = sem("hot_ready")
        count_done = sem("count_done")
        counts_ready = sem("counts_ready")
        base_done = sem("base_done")
        start_ready = sem("start_ready")
        start_out = sem("start_out")
        start_in = sem("start_in")
        rows_ready = sem("rows_ready")
        win_in = sem("win_in")
        tables_ready = sem("tables_ready")
        tables_out = sem("tables_out")
        col_done = sem("col_done")
        col_free = sem("col_free")
        prep_link = sem("prep_link")
        fullest_ready = sem("fullest_ready")
        fullest_turned = sem("fullest_turned")
        fits_ready = sem("fits_ready")

        def prep_sync(sp):
            sp.dma_start(dst_i[:], dst_cols).then_inc(dst_in, 16)
            for tile, source in ((w_src_s, w_src), (w_dst_s, w_dst), (w_out_s, w_out), (dp_s, dp_w)):
                sp.dma_start(tile[:], source).then_inc(const_in, 16)
            for tile, source in ((psi_dst_s, psi_dst), (psi_src_s, psi_src), (phi_x_s, phi_x), (phi_agg_s, phi_agg)):
                for l in range(LAYERS):
                    sp.dma_start(tile[:, l, :], source[l]).then_inc(const_in, 16)
            for l in range(LAYERS):
                sp.dma_start(psi_b_bc[:, l, :], psi_b[l:l + 1, :].partition_broadcast(128)).then_inc(const_in, 16)
            sp.dma_start(phi_b_col[:], phi_b).then_inc(const_in, 16)
            for tile, source in ((attn_bc, attn), (gamma_bc, gamma), (beta_bc, beta), (bout_bc, b_out), (dpb_bc, dp_b)):
                sp.dma_start(tile[:], source.partition_broadcast(128)).then_inc(const_in, 16)

        def tables_sync(sp):
            sp.wait_ge(tables_ready, 1)
            sp.dma_start(masks_d.rearrange("(p g) m s -> p (g m s)", g=GG), masks[:].rearrange("p g m s -> p (g m s)")).then_inc(tables_out, 16)
            sp.dma_start(dloc_d.rearrange("(p g) s -> p (g s)", g=GG), dloc_r[:].rearrange("p g s -> p (g s)")).then_inc(tables_out, 16)
            sp.wait_ge(tables_out, 32)
            sp.wait_ge(const_in, ALL_CONSTS)
            sp.wait_ge(col_free, 3 * GG)

        def prep_gpsimd(pool):
            nc.gpsimd.iota(iota_i[:], [[1, 128]], 0, 0).then_inc(iota_made, 1)
            nc.gpsimd.iota(iota_ci[:], [[0, 1]], 0, 1).then_inc(iota_made, 1)
            nc.gpsimd.iota(base_i[:], [[NB, GG]], 0, NB * GG).then_inc(iota_made, 1)
            pool.wait_ge(start_ready, 1)
            pool.dma_start(start_d, start_q[:]).then_inc(start_out, 16)
            pool.wait_ge(start_out, 16)
            pool.dma_start(start_s[:], start_d.rearrange("q r -> (q r)").rearrange("(p g) -> p g", g=GG)).then_inc(start_in, 16)
            pool.wait_ge(rows_ready, 1)
            for g in range(GG):
                for r in range(2):
                    nc.gpsimd.indirect_dma_start(
                        win_i[:, g, r, :, :].rearrange("p k s -> p (k s)"), None, src_dst,
                        bass.IndirectOffsetOnAxis(ap=row_i[:, r, g:g + 1], axis=0)).then_inc(win_in, 16)

        def prep_vector(dve):
            made = [0]

            def link(ins):
                made[0] += 1
                ins.then_inc(prep_link, 1)
                dve.wait_ge(prep_link, made[0])

            v = nc.vector
            dve.wait_ge(iota_made, 3)
            link(v.tensor_copy(iota_row[:], iota_i[:]))
            link(v.tensor_copy(iota_col[:], iota_ci[:]))
            link(v.memset(eps_col[:], EPS))
            link(v.memset(tiny_col[:], 1e-8))
            link(v.memset(one_col[:], 1.0))
            link(v.tensor_copy(base_f[:], base_i[:]))
            v.tensor_scalar(ident[:], iota_row[:], iota_col[:, 0:1], None, ALU.is_equal).then_inc(const_made, 1)
            link(v.tensor_scalar(upper[:], iota_row[0:QN, 0:QN], iota_col[0:QN, 0:1], None, ALU.is_gt))
            dve.wait_ge(dst_in, 16)
            link(v.tensor_copy(dst_f[:], dst_i[:]))
            link(v.tensor_scalar(quot[:], dst_f[:], float(NB * QN), None, ALU.is_ge))
            for q in range(2, QN):
                link(v.scalar_tensor_tensor(quot[:], dst_f[:], float(NB * QN * q), quot[:], ALU.is_ge, ALU.add))
            link(v.scalar_tensor_tensor(resid[:], quot[:], -float(NB * QN), dst_f[:], ALU.mult, ALU.add))
            link(v.tensor_scalar(resid[:], resid[:], 1.0 / NB, None, ALU.mult))
            link(v.tensor_tensor(is_q[:], quot[:].unsqueeze(2).broadcast_to([GP, EC, QN]),
                                 iota_row[0:GP, 0:QN].unsqueeze(1).broadcast_to([GP, EC, QN]), ALU.is_equal))
            v.tensor_tensor(is_below[:], resid[:].unsqueeze(2).broadcast_to([GP, EC, QN + 1]),
                            iota_row[0:GP, 0:QN + 1].unsqueeze(1).broadcast_to([GP, EC, QN + 1]),
                            ALU.is_lt).then_inc(hot_ready, 1)
            dve.wait_ge(count_done, 1)
            v.tensor_copy(counts[:], wide[0][0:QN, 0:QN + 1]).then_inc(counts_ready, 1)
            dve.wait_ge(counts_ready, 1)
            dve.wait_ge(base_done, 1)
            v.tensor_scalar(start_q[:], counts[:, 0:QN], wide[1][0:QN, 0:1], None, ALU.add).then_inc(start_ready, 1)
            link(v.tensor_tensor(filled[:], counts[:, 1:QN + 1], counts[:, 0:QN], ALU.subtract))
            v.tensor_reduce(fullest[:], filled[:], AXIS.X, ALU.max).then_inc(fullest_ready, 1)
            dve.wait_ge(fullest_turned, 1)
            link(v.tensor_reduce(fullest_row[:], bank[2][0:1, 0:QN], AXIS.X, ALU.max))
            link(v.tensor_scalar(fits_f[:], fullest_row[:], float(SLOTS), None, ALU.is_le))
            v.tensor_copy(fits_i[:], fits_f[:]).then_inc(fits_ready, 1)
            dve.wait_ge(start_in, 16)
            link(v.tensor_copy(start_i[:], start_s[:]))
            link(v.tensor_scalar(row_i[:, 0, :], start_i[:], 7, None, ALU.logical_shift_right))
            link(v.tensor_scalar(rot_i[:], start_i[:], SLOTS - 1, None, ALU.bitwise_and))
            v.tensor_scalar(row_i[:, 1, :], row_i[:, 0, :], 1, None, ALU.add).then_inc(rows_ready, 1)
            for b in range(7):
                link(v.tensor_scalar(bit_i[:, b, :], rot_i[:], b, 1, ALU.logical_shift_right, ALU.bitwise_and))
            link(v.tensor_copy(bit_f[:], bit_i[:].unsqueeze(3).broadcast_to([GP, 7, GG, 2])))
            dve.wait_ge(win_in, 16 * 2 * GG)
            for r in range(2):
                link(v.tensor_copy(win[0][:, :, :, r * SLOTS:(r + 1) * SLOTS], win_i[:, :, r, :, :]))
            left, at = 2 * SLOTS, 0
            for b in range(6, -1, -1):
                left -= 1 << b
                now = win[at][:].rearrange("p g k s -> p (g k) s")
                new = win[1 - at][:].rearrange("p g k s -> p (g k) s")
                dif = step[:].rearrange("p g k s -> p (g k) s")[:, :, 0:left]
                bits = bit_f[:, b, :, :].rearrange("p g k -> p (g k)").unsqueeze(2).broadcast_to([GP, 2 * GG, left])
                link(v.tensor_tensor(dif, now[:, :, (1 << b):(1 << b) + left], now[:, :, 0:left], ALU.subtract))
                link(v.tensor_tensor(dif, dif, bits, ALU.mult))
                link(v.tensor_tensor(new[:, :, 0:left], dif, now[:, :, 0:left], ALU.add))
                at = 1 - at
            src_w, dst_w = win[at][:, :, 0, 0:SLOTS], win[at][:, :, 1, 0:SLOTS]
            link(v.tensor_copy(src_r[:], src_w))
            link(v.tensor_tensor(dloc_r[:], dst_w, base_f[:].unsqueeze(2).broadcast_to([GP, GG, SLOTS]), ALU.subtract))
            link(v.memset(masks[:], 0.0))
            link(v.memset(ones_r[:], 1.0))
            link(v.tensor_tensor(masks[:, :, 2, 1:], dloc_r[:, :, 1:], dloc_r[:, :, 0:SLOTS - 1], ALU.is_equal))
            link(v.tensor_tensor(masks[:, :, 3, 0:SLOTS - 1], dloc_r[:, :, 1:], dloc_r[:, :, 0:SLOTS - 1], ALU.is_equal))
            link(v.tensor_scalar(masks[:, :, 0:2, :], masks[:, :, 2:4, :], BIG, -BIG, ALU.mult, ALU.add))
            for g in range(GG):
                link(v.tensor_tensor_scan(cnt_f[:, g, :], masks[:, g, 2, :], ones_r[:], 0.0, ALU.mult, ALU.add))
                link(v.tensor_tensor_scan(deg_r[:, g, ::-1], masks[:, g, 3, ::-1], cnt_f[:, g, ::-1], 0.0, ALU.mult, ALU.max))
            v.reciprocal(invdeg_r[:], deg_r[:]).then_inc(tables_ready, 1)
            n = 0
            for g in range(GG):
                for table in (dloc_c, invdeg_c, src_c):
                    dve.wait_ge(col_done, n + 1)
                    v.tensor_copy(table[:, g::GG], bank[2 + n % 2][:, 0:GP]).then_inc(col_free, 1)
                    n += 1

        def prep_tensor(pe):
            pe.wait_ge(hot_ready, 1)
            for c in range(EC):
                last = nc.tensor.matmul(wide[0][0:QN, 0:QN + 1], is_q[:, c, :], is_below[:, c, :],
                                        start=(c == 0), stop=(c == EC - 1))
            last.then_inc(count_done, 1)
            pe.wait_ge(counts_ready, 1)
            nc.tensor.matmul(wide[1][0:QN, 0:1], upper[:], counts[:, QN:QN + 1], start=True, stop=True).then_inc(base_done, 1)
            pe.wait_ge(fullest_ready, 1)
            pe.wait_ge(const_made, 1)
            nc.tensor.transpose(bank[2][0:1, 0:QN], fullest[:], ident[0:QN, 0:QN]).then_inc(fullest_turned, 1)

        def columns_tensor(pe):
            pe.wait_ge(tables_ready, 1)
            n = 0
            for g in range(GG):
                for table in (dloc_r, invdeg_r, src_r):
                    wait(pe, col_free, n - 1)
                    nc.tensor.transpose(bank[2 + n % 2][:, 0:GP], table[:, g, :], ident[0:GP, 0:GP]).then_inc(col_done, 1)
                    n += 1

        xt_in = sb("xt_in", [D, 3, TN])
        hs_out = sb("hs_out", [TP, 3, TT, D])
        t_in = [sem(f"t_in{s}") for s in range(3)]
        t_out = [sem(f"t_out{s}") for s in range(3)]
        t_mm = sem("t_mm")
        t_ev = sem("t_ev")

        def rows_of(table, i):
            return table[bass.ds(i.n(0, TN), TN), :].rearrange("(t p) d -> p t d", p=TP)

        def table_sync(sp):
            def body(i):
                if i.live():
                    wait(sp, t_mm, i.n(-2))
                    sp.dma_start(xt_in[:, i.slot(3), :], xT[:, bass.ds(i.n(0, TN), TN)]).then_inc(t_in[i.slot(3)], 16)
                k = i.back(3)
                if k.live():
                    sp.wait_ge(t_ev, k.n(1))
                    sp.dma_start(rows_of(hs_table, k), hs_out[:, k.slot(3), :, :]).then_inc(t_out[k.slot(3)], 16)
            walk(sp, body, TILES, 3)
            for s in range(3):
                sp.wait_ge(t_out[s], 16 * len(range(s, TILES, 3)))

        def table_tensor(pe):
            pe.wait_ge(const_in, ALL_CONSTS)

            def body(i):
                if i.live():
                    pe.wait_ge(t_in[i.slot(3)], i.use(3, 1) * 16)
                    wait(pe, t_ev, i.n(-1))
                    for t in range(TT):
                        last = nc.tensor.matmul(bank[i.slot(2)][0:TP, t * D:(t + 1) * D],
                                                xt_in[:, i.slot(3), t * TP:(t + 1) * TP], w_src_s[:], start=True, stop=True)
                    last.then_inc(t_mm, 1)
            walk(pe, body, TILES, 0, pause=3, meanwhile=lambda: prep_tensor(pe))

        def table_scalar(act):
            def body(i):
                if i.live():
                    act.wait_ge(t_mm, i.n(1))
                    wait(act, t_out[i.slot(3)], i.use(3) * 16)
                    nc.scalar.copy(hs_out[:, i.slot(3), :, :].rearrange("p t d -> p (t d)"),
                                   bank[i.slot(2)][0:TP, :]).then_inc(t_ev, 1)
            walk(act, body, TILES, 0)

        give_back()

        own_space()
        o_in = sb("o_in", [D, TN])
        o_rows = sb("o_rows", [TP, TT, D])
        o_resid = sb("o_resid", [TP, TT, D])
        o_T = sb("o_T", [D, TN])
        o_agg = sb("o_agg", [D, TN])
        o_st = sb("o_st", [TP, TT, 6])
        o_mv = sb("o_mv", [TP, 1, TT, 2])
        o_log = sb("o_log", [TP, 1, TT])
        o_rs = sb("o_rs", [TP, 1, TT])
        o_sh = sb("o_sh", [TP, 1, TT])
        e_src = sb("e_src", [TP, 1], I32)
        e_ints = sb("e_ints", [TP, 3], I32)
        e_row_i = sb("e_row_i", [TP, 2, TP], I32)
        e_cols = sb("e_cols", [TP, 3])
        e_row = sb("e_row", [TP, 2, TP])
        e_more = sb("e_more", [TP, 1])
        e_put_f = sb("e_put_f", [TP, 1])
        e_put = sb("e_put", [TP, 1], I32)
        is_last = sb("is_last", [TP, 1])
        same = sb("same", [TP, TP])
        carry_on = sb("carry_on", [TP, TP])
        src_rows = sb("src_rows", [TP, D])
        dst_rows = sb("dst_rows", [TP, D])
        max_rows = sb("max_rows", [TP, H])
        e_pre = sb("e_pre", [TP, D])
        e_leaky = sb("e_leaky", [TP, D])
        e_prod = sb("e_prod", [TP, D])
        e_score = sb("e_score", [TP, H])
        e_keep = sb("e_keep", [H, TP])
        e_pen = sb("e_pen", [H, TP])
        e_sT = sb("e_sT", [H, TP])
        e_run = sb("e_run", [H, TP])
        e_last = sb("e_last", [H, 1])
        e_shift = sb("e_shift", [TP, H])
        e_max = sb("e_max", [TP, H])
        e_terms = sb("e_terms", [TP, D + H])
        e_total = sb("e_total", [TP, D + H])
        e_den = sb("e_den", [TP, H])
        e_inv = sb("e_inv", [TP, H])
        e_out = sb("e_out", [TP, D])
        give_back()

        x_in = [sem(f"x_in{s}") for s in range(UNROLL)]
        dl_in = [sem(f"dl_in{s}") for s in range(3)]
        rows_in = [sem(f"rows_in{s}") for s in range(UNROLL)]
        cols_out = [sem(f"cols_out{s}") for s in range(UNROLL)]
        g_yo = [sem(f"g_yo{s}") for s in range(UNROLL)]
        g_x1 = [sem(f"g_resid{s}") for s in range(3)]
        (g_idx, g_slot1h, g_node1h, g_z, g_zev, g_u, g_pre, g_m, g_agg, g_aggev, g_q, g_relu, g_xnew, g_y, g_yev,
         f_sum, f_st, f_mv, f_log, f_rstd, f_sh) = [sem(s) for s in (
             "g_idx", "g_slot1h", "g_node1h", "g_z", "g_zev", "g_u", "g_pre", "g_m", "g_agg", "g_aggev", "g_q", "g_relu", "g_xnew",
             "g_y", "g_yev", "f_sum", "f_st", "f_mv", "f_log", "f_rstd", "f_sh")]
        paired = iter([g_idx, g_slot1h, g_node1h, g_z, g_zev, g_u, g_pre, g_m, g_agg, g_aggev, g_q, g_relu, g_xnew, g_y, g_yev,
                       f_sum, f_st, f_mv, f_log, f_rstd, f_sh, *cols_out, *g_yo])
        name_of = {}

        def twin(name):
            handle = next(paired)
            name_of[handle.num] = name
            return handle

        o_loaded, o_product, o_copied, o_stored, o_relu, o_sum, o_stat, o_mvs, o_logs, o_rstd, o_shs = [twin(s) for s in (
            "o_loaded", "o_product", "o_copied", "o_stored", "o_relu", "o_sum", "o_stat", "o_mvs", "o_logs", "o_rstd", "o_shs")]
        e_loaded, e_gathered, e_indexed, e_link, e_scored, e_terms_in, e_turned, e_ran, e_shifted, e_probs, e_result, e_scattered, e_kept = [
            twin(s) for s in ("e_loaded", "e_gathered", "e_indexed", "e_link", "e_scored", "e_terms_in", "e_turned", "e_ran",
                             "e_shifted", "e_probs", "e_result", "e_scattered", "e_kept")]
        zero_made = sem("zero_made")
        zero_out = sem("zero_out")

        hd_table = dram("hd_table", [N, D])
        max_table = dram("max_table", [N, H])
        score_d = dram("score_d", [E, H])
        att_rows = dram("att_rows", [N, D])
        agrows_in = dram("agrows_in", [N, D])
        aggT_d = dram("aggT_d", [D, N])
        fin_rows = dram("fin_rows", [N, D])
        xT_last = dram("xT_last", [D, N])

        def tile_rows(table, t):
            return table[bass.ds(t * TN, TN), :].rearrange("(t p) d -> p t d", p=TP)

        def tile_cols(table, t):
            return table[:, bass.ds(t * TN, TN)]

        NODE_RATES = {
            "table": {"o_loaded": 16, "o_product": 1, "o_copied": 1, "o_stored": 16},
            "turn": {"o_loaded": 16, "o_product": 1, "o_copied": 1, "o_stored": 16},
            "update": {"o_loaded": 32, "o_product": 1, "o_relu": 1, "o_copied": 1, "o_stored": 16},
            "final": {"o_loaded": 32, "o_sum": 1, "o_stat": 1, "o_mvs": 1, "o_logs": 1, "o_rstd": 1, "o_shs": 1,
                      "o_copied": 1, "o_stored": 16},
        }
        LINKS = {"scores": 11, "attend": 9, "mean": 9}
        EDGE_RATES = {
            "scores": {"e_loaded": 96, "e_gathered": 32, "e_indexed": 1, "e_link": LINKS["scores"], "e_scored": 1, "e_turned": 2,
                       "e_ran": 1, "e_result": 1, "e_scattered": 16, "e_kept": 16},
            "attend": {"e_loaded": 112, "e_gathered": 32, "e_indexed": 1, "e_link": LINKS["attend"], "e_shifted": 1, "e_probs": 1,
                       "e_terms_in": 1, "e_turned": 1, "e_result": 1, "e_scattered": 16},
            "mean": {"e_loaded": 96, "e_gathered": 32, "e_indexed": 1, "e_link": LINKS["mean"], "e_terms_in": 1, "e_turned": 1,
                     "e_result": 1, "e_scattered": 16},
        }

        def counted(plan, at):
            tiles = {**{k: TILES for k in NODE_RATES}, **{k: EC for k in EDGE_RATES}}
            rates = {**NODE_RATES, **EDGE_RATES}

            def after(s, t, k):
                base = sum(rates[p[0]].get(name_of[s.num], 0) * tiles[p[0]] for p in plan[:at])
                return t * rates[plan[at][0]][name_of[s.num]] + (base + k)
            return after

        def node_sync(sp, after, kind, source, dest, second=None, **_):
            with sp.Fori(0, TILES) as t:
                if kind in ("table", "update"):
                    sp.dma_start(o_in[:], tile_cols(source, t)).then_inc(o_loaded, 16)
                else:
                    sp.dma_start(o_rows[:], tile_rows(source, t)).then_inc(o_loaded, 16)
                if kind == "update":
                    sp.dma_start(o_agg[:], tile_cols(second, t)).then_inc(o_loaded, 16)
                if kind == "final":
                    sp.dma_start(o_resid[:], tile_rows(second, t)).then_inc(o_loaded, 16)
                sp.wait_ge(o_copied, after(o_copied, t, 1))
                apart(sp)
                if kind in ("table", "final"):
                    sp.dma_start(tile_rows(dest, t), o_rows[:]).then_inc(o_stored, 16)
                else:
                    sp.dma_start(tile_cols(dest, t), o_T[:]).then_inc(o_stored, 16)
                sp.wait_ge(o_stored, after(o_stored, t, 16))
                apart(sp)

        def node_tensor(pe, after, kind, weight=None, l=0, **_):
            if kind == "final":
                return
            with pe.Fori(0, TILES) as t:
                pe.wait_ge(o_loaded, after(o_loaded, t, NODE_RATES[kind]["o_loaded"]))
                apart(pe)
                if kind == "table":
                    for c in range(TT):
                        last = nc.tensor.matmul(bank[0][0:TP, c * D:(c + 1) * D], o_in[:, c * TP:(c + 1) * TP], weight, start=True, stop=True)
                elif kind == "turn":
                    for c in range(TT):
                        last = nc.tensor.transpose(bank[0][:, c * TP:(c + 1) * TP], o_rows[:, c, :], ident[0:TP, 0:TP])
                else:
                    nc.tensor.matmul(bank[0][:, 0:TN], phi_x_s[:, l, :], o_in[:], start=True, stop=False)
                    last = nc.tensor.matmul(bank[0][:, 0:TN], phi_agg_s[:, l, :], o_agg[:], start=False, stop=True)
                last.then_inc(o_product, 1)

        def node_scalar(act, after, kind, l=0, **_):
            if kind not in ("update", "final"):
                return
            with act.Fori(0, TILES) as t:
                if kind == "update":
                    act.wait_ge(o_product, after(o_product, t, 1))
                    nc.scalar.activation(o_T[:], bank[0][:, 0:TN], ACT.Relu, bias=phi_b_col[:, l:l + 1]).then_inc(o_relu, 1)
                else:
                    act.wait_ge(o_mvs, after(o_mvs, t, 1))
                    nc.scalar.activation(o_log[:, 0, :], o_mv[:, 0, :, 1], ACT.Ln, bias=eps_col[0:TP, 0:1]).then_inc(o_logs, 1)
                    act.wait_ge(o_logs, after(o_logs, t, 1))
                    nc.scalar.activation(o_rs[:, 0, :], o_log[:, 0, :], ACT.Exp, scale=-0.5).then_inc(o_rstd, 1)
                    act.wait_ge(o_shs, after(o_shs, t, 1))
                    for c in range(TT):
                        last = nc.scalar.activation(o_rows[:, c, :], o_resid[:, c, :], ACT.Identity,
                                                    bias=o_sh[:, 0, c:c + 1], scale=o_rs[:, 0, c:c + 1])
                    last.then_inc(o_copied, 1)

        def node_vector(dve, after, kind, bias=None, **_):
            v = nc.vector
            with dve.Fori(0, TILES) as t:
                if kind == "table":
                    dve.wait_ge(o_product, after(o_product, t, 1))
                    if bias is None:
                        v.tensor_copy(flat(o_rows[:]), bank[0][0:TP, :]).then_inc(o_copied, 1)
                    else:
                        v.tensor_tensor(o_rows[:], bank[0][0:TP, :].rearrange("p (t d) -> p t d", d=D),
                                        bias.unsqueeze(1).broadcast_to([TP, TT, D]), ALU.add).then_inc(o_copied, 1)
                elif kind == "turn":
                    dve.wait_ge(o_product, after(o_product, t, 1))
                    v.tensor_copy(o_T[:], bank[0][:, 0:TN]).then_inc(o_copied, 1)
                elif kind == "update":
                    dve.wait_ge(o_relu, after(o_relu, t, 1))
                    v.tensor_tensor(o_T[:], o_T[:], o_in[:], ALU.add).then_inc(o_copied, 1)
                else:
                    dve.wait_ge(o_loaded, after(o_loaded, t, 32))
                    v.tensor_tensor(o_resid[:], o_resid[:], o_rows[:], ALU.add).then_inc(o_sum, 1)
                    dve.wait_ge(o_sum, after(o_sum, t, 1))
                    for c in range(TT):
                        last = v.bn_stats(o_st[:, c, :], o_resid[:, c, :])
                    last.then_inc(o_stat, 1)
                    dve.wait_ge(o_stat, after(o_stat, t, 1))
                    apart(dve)
                    for c in range(TT):
                        last = v.bn_aggr(o_mv[:, 0, c, :], o_st[:, c, :])
                    last.then_inc(o_mvs, 1)
                    dve.wait_ge(o_rstd, after(o_rstd, t, 1))
                    v.scalar_tensor_tensor(o_sh[:, 0, :], o_mv[:, 0, :, 0], -1.0, o_rs[:, 0, :], ALU.mult, ALU.mult).then_inc(o_shs, 1)

        def edge_sync(sp, after, kind, **_):
            with sp.Fori(0, EC) as t:
                sp.dma_start(e_src[:], src_flat[bass.ds(t * TP, TP), :]).then_inc(e_loaded, 16)
                sp.dma_start(e_ints[:, 0:1], dst_pad[bass.ds(t * TP + 1, TP), :]).then_inc(e_loaded, 16)
                sp.dma_start(e_ints[:, 1:2], dst_pad[bass.ds(t * TP + 2, TP), :]).then_inc(e_loaded, 16)
                sp.dma_start(e_ints[:, 2:3].unsqueeze(1), dst_pad[bass.ds(t * TP, 1), :].rearrange("a b -> (a b)").partition_broadcast(TP)).then_inc(e_loaded, 16)
                for r in range(2):
                    sp.dma_start(e_row_i[:, r, :].unsqueeze(1), dst_pad[bass.ds(t * TP + (1 - r), TP), :].rearrange("a b -> (a b)").partition_broadcast(TP)
                                 ).then_inc(e_loaded, 16)
                if kind == "attend":
                    sp.dma_start(e_score[:], score_d[bass.ds(t * TP, TP), :]).then_inc(e_loaded, 16)
                if kind == "scores":
                    sp.wait_ge(e_scored, after(e_scored, t, 1))
                    sp.dma_start(score_d[bass.ds(t * TP, TP), :], e_score[:]).then_inc(e_kept, 16)
                    sp.wait_ge(e_kept, after(e_kept, t, 16))
                sp.wait_ge(e_scattered, after(e_scattered, t, 16))
                apart(sp)

        def edge_gpsimd(pool, after, kind, src_table, dst_table, dest):
            with pool.Fori(0, EC) as t:
                pool.wait_ge(e_indexed, after(e_indexed, t, 1))
                apart(pool)
                nc.gpsimd.indirect_dma_start(src_rows[:], None, src_table, bass.IndirectOffsetOnAxis(ap=e_src[:, 0:1], axis=0)).then_inc(e_gathered, 16)
                nc.gpsimd.indirect_dma_start(max_rows[:] if kind == "attend" else dst_rows[:], None, dst_table,
                                             bass.IndirectOffsetOnAxis(ap=e_ints[:, 0:1], axis=0)).then_inc(e_gathered, 16)
                pool.wait_ge(e_result, after(e_result, t, 1))
                apart(pool)
                nc.gpsimd.indirect_dma_start(dest, bass.IndirectOffsetOnAxis(ap=e_put[:, 0:1], axis=0),
                                             e_max[:] if kind == "scores" else e_out[:], None,
                                             bounds_check=N - 1, oob_is_err=False).then_inc(e_scattered, 16)
                pool.wait_ge(e_scattered, after(e_scattered, t, 16))

        def edge_tensor(pe, after, kind, **_):
            w = D + H if kind == "attend" else D + 1
            with pe.Fori(0, EC) as t:
                if kind == "scores":
                    pe.wait_ge(e_scored, after(e_scored, t, 1))
                    apart(pe)
                    nc.tensor.transpose(bank[0][0:H, 0:TP], e_score[:], ident[0:TP, 0:TP]).then_inc(e_turned, 1)
                    pe.wait_ge(e_ran, after(e_ran, t, 1))
                    apart(pe)
                    nc.tensor.transpose(bank[1][0:TP, 0:H], e_run[:], ident[0:H, 0:H]).then_inc(e_turned, 1)
                else:
                    pe.wait_ge(e_terms_in, after(e_terms_in, t, 1))
                    nc.tensor.matmul(bank[0][0:TP, 0:w], same[:], e_terms[:, 0:w], start=True, stop=False)
                    nc.tensor.matmul(bank[0][0:TP, 0:w], carry_on[:], e_total[:, 0:w], start=False, stop=True).then_inc(e_turned, 1)

        def edge_scalar(act, after, kind, **_):
            if kind == "attend":
                with act.Fori(0, EC) as t:
                    act.wait_ge(e_shifted, after(e_shifted, t, 1))
                    nc.scalar.activation(e_terms[:, D:D + H], e_shift[:], ACT.Exp).then_inc(e_probs, 1)

        def edge_vector(dve, after, kind, **_):
            v = nc.vector
            w = D + H if kind == "attend" else D + 1
            if kind == "mean":
                v.memset(e_terms[:, D:D + 1], 1.0)
            with dve.Fori(0, EC) as t:
                done = [0]

                def link(ins):
                    done[0] += 1
                    ins.then_inc(e_link, 1)
                    dve.wait_ge(e_link, after(e_link, t, done[0]))

                dve.wait_ge(e_loaded, after(e_loaded, t, EDGE_RATES[kind]["e_loaded"]))
                link(v.tensor_copy(e_cols[:], e_ints[:]))
                link(v.tensor_copy(e_row[:], e_row_i[:]))
                link(v.tensor_tensor(e_more[:], e_cols[:, 0:1], e_cols[:, 1:2], ALU.is_equal))
                link(v.scalar_tensor_tensor(e_put_f[:], e_more[:], float(1 << 20), e_cols[:, 0:1], ALU.mult, ALU.add))
                v.tensor_copy(e_put[:], e_put_f[:]).then_inc(e_indexed, 1)
                if kind != "scores":
                    link(v.tensor_scalar(same[:], e_row[:, 0, :], e_cols[:, 0:1], None, ALU.is_equal))
                    link(v.tensor_scalar(carry_on[:], e_row[:, 0, :], e_cols[:, 2:3], is_last[:, 0:1], ALU.is_equal, ALU.mult))
                dve.wait_ge(e_gathered, after(e_gathered, t, 32))
                if kind != "attend":
                    link(v.tensor_tensor(e_pre[:], src_rows[:], dst_rows[:], ALU.add))
                if kind == "scores":
                    link(v.scalar_tensor_tensor(e_leaky[:], e_pre[:], 0.2, e_pre[:], ALU.mult, ALU.max))
                    link(v.tensor_tensor(e_prod[:], e_leaky[:], attn_bc[0:TP, :], ALU.mult))
                    v.tensor_reduce(e_score[:], e_prod[:].rearrange("p (h d) -> p h d", d=HD), AXIS.X, ALU.add).then_inc(e_scored, 1)
                    link(v.tensor_tensor(e_keep[:], e_row[0:H, 0, :], e_row[0:H, 1, :], ALU.is_equal))
                    link(v.tensor_scalar(e_pen[:], e_keep[:], BIG, -BIG, ALU.mult, ALU.add))
                    dve.wait_ge(e_turned, after(e_turned, t, 1))
                    link(v.tensor_copy(e_sT[:], bank[0][0:H, 0:TP]))
                    link(v.tensor_tensor_scan(e_run[:], e_pen[:], e_sT[:], e_last[:, 0:1], ALU.add, ALU.max))
                    v.tensor_copy(e_last[:], e_run[:, TP - 1:TP]).then_inc(e_ran, 1)
                    dve.wait_ge(e_turned, after(e_turned, t, 2))
                    v.tensor_copy(e_max[:], bank[1][0:TP, 0:H]).then_inc(e_result, 1)
                if kind == "attend":
                    v.tensor_tensor(e_shift[:], e_score[:], max_rows[:], ALU.subtract).then_inc(e_shifted, 1)
                    dve.wait_ge(e_probs, after(e_probs, t, 1))
                    v.tensor_tensor(e_terms[:, 0:D].rearrange("p (h d) -> p h d", d=HD), src_rows[:].rearrange("p (h d) -> p h d", d=HD),
                                    e_terms[:, D:D + H].unsqueeze(2).broadcast_to([TP, H, HD]), ALU.mult).then_inc(e_terms_in, 1)
                if kind == "mean":
                    v.tensor_scalar(e_terms[:, 0:D], e_pre[:], 0.0, None, ALU.max).then_inc(e_terms_in, 1)
                if kind != "scores":
                    dve.wait_ge(e_turned, after(e_turned, t, 1))
                    link(v.tensor_copy(e_total[:, 0:w], bank[0][0:TP, 0:w]))
                if kind == "attend":
                    link(v.tensor_scalar(e_den[:], e_total[:, D:D + H], 1e-8, None, ALU.add))
                    link(v.reciprocal(e_inv[:], e_den[:]))
                    v.tensor_tensor(e_out[:].rearrange("p (h d) -> p h d", d=HD), e_total[:, 0:D].rearrange("p (h d) -> p h d", d=HD),
                                    e_inv[:].unsqueeze(2).broadcast_to([TP, H, HD]), ALU.mult).then_inc(e_result, 1)
                if kind == "mean":
                    link(v.reciprocal(e_inv[:, 0:1], e_total[:, D:D + 1]))
                    v.tensor_scalar(e_out[:], e_total[:, 0:D], e_inv[:, 0:1], None, ALU.mult).then_inc(e_result, 1)
                assert done[0] == LINKS[kind], (kind, done[0])

        ATTEND = [
            ("table", dict(source=xT, weight=w_dst_s[:], dest=hd_table)),
            ("scores", dict(src_table=hs_table, dst_table=hd_table, dest=max_table)),
            ("attend", dict(src_table=hs_table, dst_table=max_table, dest=att_rows)),
            ("turn", dict(source=att_rows, dest=attT)),
        ]
        LAYER_PLAN = []
        xs = xT_l + [xT_last]
        for l in range(LAYERS):
            LAYER_PLAN += [
                ("table", dict(source=xs[l], weight=psi_dst_s[:, l, :], bias=psi_b_bc[0:TP, l, :], dest=hd_table)),
                ("mean", dict(src_table=y_table[l], dst_table=hd_table, dest=agrows_in)),
                ("turn", dict(source=agrows_in, dest=aggT_d)),
                ("update", dict(source=xs[l], second=aggT_d, l=l, dest=xs[l + 1])),
            ]
            if l < LAYERS - 1:
                LAYER_PLAN += [("table", dict(source=xs[l + 1], weight=psi_src_s[:, l + 1, :], dest=y_table[l + 1]))]
        LAYER_PLAN += [("table", dict(source=xT_last, weight=dp_s[:], dest=fin_rows)),
                       ("final", dict(source=fin_rows, second=resid_rows, dest=out))]
        PLAN = ATTEND + LAYER_PLAN

        def general(eng, node, edge, first, end):
            for at in range(first, end):
                kind, what = PLAN[at]
                program = node if kind in NODE_RATES else edge
                if program:
                    program(eng, counted(PLAN, at), kind, **what)

        def zero_sync(sp):
            sp.wait_ge(zero_made, 1)
            with sp.Fori(0, TILES) as t:
                for table in (att_rows, agrows_in):
                    sp.dma_start(tile_rows(table, t), o_rows[:]).then_inc(zero_out, 16)
                sp.dma_start(tile_rows(max_table, t), o_rows[:, :, 0:H]).then_inc(zero_out, 16)
            sp.wait_ge(zero_out, 16 * 3 * TILES)

        def zero_vector(dve):
            v = nc.vector
            v.memset(e_total[:], 0.0)
            v.memset(e_last[:], -BIG)
            v.tensor_scalar(is_last[:], iota_col[0:TP, :], float(TP - 1), None, ALU.is_equal)
            v.memset(o_rows[:], 0.0).then_inc(zero_made, 1)

        def by_path(eng, fast, slow):
            eng.wait_ge(fits_ready, 1)
            fits = eng.value_load(fits_i[0:1, 0:1], min_val=0, max_val=1)
            with eng.If(fits > 0):
                fast()
            with eng.Else():
                slow()

        xt_b = sb("xt_b", [D, UNROLL, BN])
        dl_b = sb("dl_b", [NB, 3, BS])
        mask_b = sb("mask_b", [K * H, 3, 4, SLOTS])
        idx_b = sb("idx_b", [SLOTS, UNROLL, K], I32)
        rows_b = sb("rows_b", [SLOTS, UNROLL, K, D])
        hd_b = sb("hd_b", [NB, 2, BS])
        to_slot = sb("to_slot", [NB, 2, BS])
        to_node = sb("to_node", [SLOTS, 2, K, NB])
        pre_b = sb("pre_b", [SLOTS, 2, K * D])
        fifth_b = sb("fifth_b", [SLOTS, 2, K * D])
        leaky_b = sb("leaky_b", [SLOTS, 2, K * D])
        prod_b = sb("prod_b", [SLOTS, K * D])
        score_b = sb("score_b", [SLOTS, 2, K * H])
        run_max = sb("run_max", [K * H, SLOTS])
        seg_max = sb("seg_max", [K * H, SLOTS])
        shifted = sb("shifted", [K * H, SLOTS])
        probs = sb("probs", [K * H, SLOTS])
        run_sum = sb("run_sum", [K * H, SLOTS])
        seg_sum = sb("seg_sum", [K * H, SLOTS])
        denom = sb("denom", [SLOTS, K * H])
        inv_denom = sb("inv_denom", [SLOTS, K * H])
        alpha = sb("alpha", [SLOTS, K * H])
        msg_b = sb("msg_b", [SLOTS, 2, K * D])
        att_b = sb("att_b", [D, UNROLL, BN])

        a_mask = [sem(f"a_mask{s}") for s in range(3)]
        a_idx = sem("a_idx")
        a_near = sem("a_near")
        a_denom = sem("a_denom")
        a_hd = sem("a_hd")
        a_hd_ev = sem("a_hd_ev")
        a_slot1h = sem("a_slot1h")
        a_node1h = sem("a_node1h")
        a_u = sem("a_u")
        a_fifth = sem("a_fifth")
        a_leaky = sem("a_leaky")
        a_prod = sem("a_prod")
        a_score = sem("a_score")
        a_sT = sem("a_sT")
        a_scan = sem("a_scan")
        a_weigh = sem("a_weigh")
        a_shift = sem("a_shift")
        a_exp = sem("a_exp")
        a_alpha = sem("a_alpha")
        a_alphaT = sem("a_alphaT")
        a_msg = sem("a_msg")
        a_agg = sem("a_agg")
        a_ev = sem("a_ev")
        SCANS = 3

        def uses(slots, phases):
            return [phases * len(range(s, BATCHES, slots)) for s in range(slots)]

        WEIGHS = 2

        def att_sync(sp):
            def body(i):
                if i.live():
                    wait(sp, a_hd, i.n(1 - UNROLL))
                    sp.dma_start(xt_b[:, i.slot(UNROLL), :], xT[:, bass.ds(i.n(0, BN), BN)]).then_inc(x_in[i.slot(UNROLL)], 16)
                    wait(sp, a_slot1h, i.n(-2))
                    sp.dma_start(dl_b[:, i.slot(3), :].unsqueeze(1),
                                 dloc_d[bass.ds(i.n(0, K), K), :].rearrange("k s -> (k s)").partition_broadcast(NB)
                                 ).then_inc(dl_in[i.slot(3)], 16)
                j = i.back(1)
                if j.live():
                    wait(sp, a_alpha, j.n(-2))
                    sp.dma_start(mask_b[:, j.slot(3), :, :].rearrange("p m s -> p (m s)"),
                                 masks_d[bass.ds(j.n(0, K), K), :, :].rearrange("k m s -> k (m s)").unsqueeze(1)
                                 .broadcast_to([K, H, 4 * SLOTS])).then_inc(a_mask[j.slot(3)], 16)
                k = i.back(6)
                if k.live():
                    sp.wait_ge(a_ev, k.n(1))
                    sp.dma_start(attT[:, bass.ds(k.n(0, BN), BN)], att_b[:, k.slot(UNROLL), :]).then_inc(cols_out[k.slot(UNROLL)], 16)
            walk(sp, body, BATCHES, 6)
            for s in range(UNROLL):
                sp.wait_ge(cols_out[s], 16 * len(range(s, BATCHES, UNROLL)))

        def gather(pool, i, table, idx_sem, row_sems, used, base):
            wait(pool, used, i.n(base + 1 - UNROLL) if not i.fixed or i.n() >= UNROLL else 0)
            pool.wait_ge(idx_sem, i.n(base + 1))
            apart(pool)
            for k in range(K):
                nc.gpsimd.indirect_dma_start(
                    rows_b[:, i.slot(UNROLL), k, :], None, table,
                    bass.IndirectOffsetOnAxis(ap=idx_b[:, i.slot(UNROLL), k:k + 1], axis=0)).then_inc(row_sems[i.slot(UNROLL)], 16)

        def att_gpsimd(pool):
            def body(i):
                if i.live():
                    gather(pool, i, hs_table, a_idx, rows_in, a_msg, 0)
            walk(pool, body, BATCHES, 0)

        def att_tensor(pe):
            def body(i):
                j, k, m, n = i.back(1), i.back(2), i.back(3), i.back(4)
                if j.live():
                    pe.wait_ge(a_hd_ev, j.n(1))
                    pe.wait_ge(a_slot1h, j.n(1))
                    wait(pe, a_leaky, j.n())
                    pe.wait_ge(rows_in[j.slot(UNROLL)], j.use(UNROLL, 1) * 16 * K)
                    for b in range(K):
                        nc.tensor.matmul(wide[1][:, b * D:(b + 1) * D], to_slot[:, j.slot(2), b * SLOTS:(b + 1) * SLOTS],
                                         hd_b[:, j.slot(2), b * D:(b + 1) * D], start=True, stop=False)
                        last = nc.tensor.matmul(wide[1][:, b * D:(b + 1) * D], ident[:], rows_b[:, j.slot(UNROLL), b, :],
                                                start=False, stop=True)
                    last.then_inc(a_u, 1)
                if m.live():
                    pe.wait_ge(a_alpha, m.n(1))
                    wait(pe, a_msg, m.n())
                    apart(pe)
                    nc.tensor.transpose(bank[1][:, 0:K * H], probs[:], ident[0:K * H, 0:K * H])
                    nc.tensor.transpose(bank[1][:, 64:64 + K * H], seg_sum[:], ident[0:K * H, 0:K * H]).then_inc(a_alphaT, 1)
                if k.live():
                    pe.wait_ge(a_score, k.n(1))
                    wait(pe, a_shift, k.n())
                    apart(pe)
                    nc.tensor.transpose(bank[0][0:K * H, 0:SLOTS], score_b[:, k.slot(2), :], ident[:]).then_inc(a_sT, 1)
                if i.live():
                    pe.wait_ge(x_in[i.slot(UNROLL)], i.use(UNROLL, 1) * 16)
                    wait(pe, a_hd_ev, i.n())
                    for b in range(K):
                        last = nc.tensor.matmul(wide[0][0:NB, b * D:(b + 1) * D], xt_b[:, i.slot(UNROLL), b * NB:(b + 1) * NB],
                                                w_dst_s[:], start=True, stop=True)
                    last.then_inc(a_hd, 1)
                if n.live():
                    pe.wait_ge(a_msg, n.n(1))
                    pe.wait_ge(a_node1h, n.n(1))
                    wait(pe, a_ev, n.n(-1))
                    for b in range(K):
                        last = nc.tensor.matmul(bank[2 + n.slot(2)][:, b * NB:(b + 1) * NB], msg_b[:, n.slot(2), b * D:(b + 1) * D],
                                                to_node[:, n.slot(2), b, :], start=True, stop=True)
                    last.then_inc(a_agg, 1)
            walk(pe, body, BATCHES, 4)

        def att_scalar(act):
            def body(i):
                j, k, m, n = i.back(1), i.back(2), i.back(3), i.back(4)
                if i.live():
                    act.wait_ge(dl_in[i.slot(3)], i.use(3, 1) * 16)
                    nc.scalar.activation(to_slot[:, i.slot(2), :], dl_b[:, i.slot(3), :], ACT.Square, bias=iota_col[0:NB, 0:1],
                                         scale=-1.0).then_inc(a_near, 1)
                    act.wait_ge(a_near, i.n(1))
                    nc.scalar.activation(to_slot[:, i.slot(2), :], to_slot[:, i.slot(2), :], ACT.Relu, bias=one_col[0:NB, 0:1],
                                         scale=-1.0).then_inc(a_slot1h, 1)
                if j.live():
                    act.wait_ge(a_u, j.n(1))
                    wait(act, a_leaky, j.n(-1))
                    nc.scalar.mul(fifth_b[:, j.slot(2), :], wide[1][:, 0:K * D], 0.2).then_inc(a_fifth, 1)
                if m.live():
                    act.wait_ge(a_alphaT, m.n(1))
                    wait(act, a_weigh, m.n(0, WEIGHS) - 1)
                    apart(act)
                    nc.scalar.activation(denom[:], bank[1][:, 64:64 + K * H], ACT.Identity, bias=tiny_col[:, 0:1]).then_inc(a_denom, 1)
                if i.live():
                    act.wait_ge(a_hd, i.n(1))
                    wait(act, a_u, i.n(-1))
                    nc.scalar.copy(hd_b[:, i.slot(2), :], wide[0][0:NB, 0:BS]).then_inc(a_hd_ev, 1)
                if n.live():
                    act.wait_ge(a_agg, n.n(1))
                    wait(act, cols_out[n.slot(UNROLL)], n.use(UNROLL) * 16)
                    nc.scalar.copy(att_b[:, n.slot(UNROLL), :], bank[2 + n.slot(2)][:, 0:BN]).then_inc(a_ev, 1)
                if k.live():
                    act.wait_ge(a_shift, k.n(1))
                    wait(act, a_alphaT, k.n())
                    nc.scalar.activation(probs[:], shifted[:], ACT.Exp).then_inc(a_exp, 1)
            walk(act, body, BATCHES, 4)

        def slot_one_hot(dve, i, dl_sems, used, made, base, turns):
            dve.wait_ge(dl_sems[i.slot(3)], (i.use(3, 1) + turns[i.slot(3)]) * 16)
            wait(dve, used, i.n(base - 1))
            nc.vector.tensor_scalar(to_slot[:, i.slot(2), :], dl_b[:, i.slot(3), :], iota_col[0:NB, 0:1], None,
                                    ALU.is_equal).then_inc(made, 1)

        def first_indices(idx_sem):
            nc.vector.tensor_copy(idx_b[:].rearrange("p u k -> p (u k)"), src_c[:, 0:UNROLL * K]).then_inc(idx_sem, UNROLL)

        def next_indices(b, idx_sem):
            if not b.fixed or b.n() + UNROLL < BATCHES:
                nc.vector.tensor_copy(idx_b[:, b.slot(UNROLL), :], src_c[:, bass.ds(b.n(UNROLL, K), K)]
                                      ).then_inc(idx_sem, 1)

        def att_vector(dve):
            v = nc.vector
            first_indices(a_idx)

            def body(i):
                j, k, m = i.back(1), i.back(2), i.back(3)
                s = k.slot(3)
                if j.live():
                    dve.wait_ge(a_fifth, j.n(1))
                    wait(dve, a_prod, j.n(-1))
                    v.tensor_tensor(leaky_b[:, j.slot(2), :], wide[1][:, 0:K * D], fifth_b[:, j.slot(2), :],
                                    ALU.max).then_inc(a_leaky, 1)
                if m.live():
                    dve.wait_ge(a_denom, m.n(1))
                    v.reciprocal(inv_denom[:], denom[:]).then_inc(a_weigh, 1)
                if k.live():
                    dve.wait_ge(a_sT, k.n(1))
                    dve.wait_ge(a_mask[s], k.use(3, 1) * 16)
                    v.tensor_tensor_scan(run_max[:], mask_b[:, s, 0, :], bank[0][0:K * H, 0:SLOTS], -BIG, ALU.add, ALU.max).then_inc(a_scan, 1)
                if m.live():
                    dve.wait_ge(a_weigh, m.n(0, WEIGHS) + 1)
                    v.tensor_tensor(alpha[:], bank[1][:, 0:K * H], inv_denom[:], ALU.mult).then_inc(a_weigh, 1)
                if k.live():
                    dve.wait_ge(a_scan, k.n(0, SCANS) + 1)
                    v.tensor_tensor_scan(seg_max[:, ::-1], mask_b[:, s, 1, ::-1], run_max[:, ::-1], -BIG, ALU.add, ALU.max).then_inc(a_scan, 1)
                if m.live():
                    dve.wait_ge(a_weigh, m.n(0, WEIGHS) + 2)
                    wait(dve, a_agg, m.n(-1))
                    v.tensor_tensor(msg_b[:, m.slot(2), :].rearrange("p (h d) -> p h d", d=HD),
                                    rows_b[:, m.slot(UNROLL), :, :].rearrange("p k (h d) -> p (k h) d", d=HD),
                                    alpha[:].unsqueeze(2).broadcast_to([SLOTS, K * H, HD]), ALU.mult).then_inc(a_msg, 1)
                    next_indices(m, a_idx)
                if k.live():
                    dve.wait_ge(a_scan, k.n(0, SCANS) + 2)
                    wait(dve, a_exp, k.n())
                    v.tensor_tensor(shifted[:], bank[0][0:K * H, 0:SLOTS], seg_max[:], ALU.subtract).then_inc(a_shift, 1)
                if j.live():
                    dve.wait_ge(a_leaky, j.n(1))
                    wait(dve, a_score, j.n())
                    v.tensor_tensor(prod_b[:].rearrange("p (k d) -> p k d", k=K), leaky_b[:, j.slot(2), :].rearrange("p (k d) -> p k d", k=K),
                                    attn_bc[:].unsqueeze(1).broadcast_to([SLOTS, K, D]), ALU.mult).then_inc(a_prod, 1)
                if k.live():
                    dve.wait_ge(a_exp, k.n(1))
                    v.tensor_tensor_scan(run_sum[:], mask_b[:, s, 2, :], probs[:], 0.0, ALU.mult, ALU.add).then_inc(a_scan, 1)
                if j.live():
                    dve.wait_ge(a_prod, j.n(1))
                    wait(dve, a_sT, j.n(-1))
                    v.tensor_reduce(score_b[:, j.slot(2), :], prod_b[:].rearrange("p (h d) -> p h d", d=HD),
                                    AXIS.X, ALU.add).then_inc(a_score, 1)
                if k.live():
                    dve.wait_ge(a_scan, k.n(0, SCANS) + 3)
                    wait(dve, a_alphaT, k.n())
                    v.tensor_tensor_scan(seg_sum[:, ::-1], mask_b[:, s, 3, ::-1], run_sum[:, ::-1], 0.0, ALU.mult, ALU.max).then_inc(a_alpha, 1)
                if m.live():
                    wait(dve, a_agg, m.n(-1))
                    v.tensor_tensor(to_node[:, m.slot(2), :, :], iota_row[:, 0:NB].unsqueeze(1).broadcast_to([SLOTS, K, NB]),
                                    dloc_c[:, bass.ds(m.n(0, K), K)].unsqueeze(2).broadcast_to([SLOTS, K, NB]),
                                    ALU.is_equal).then_inc(a_node1h, 1)
            walk(dve, body, BATCHES, 3)

        own_space()
        at_in = sb("at_in", [D, 3, TN])
        xr_in = sb("xr_in", [TP, 3, TT, D])
        xbout = sb("xbout", [TP, 3, TT, D])
        xbeta = sb("xbeta", [TP, UNROLL, TT, D])
        res_n = sb("res_n", [TP, 2, TT, D])
        stats = sb("stats", [TP, 2, TT, 6])
        mean_var = sb("mean_var", [TP, 2, 2, TT, 2])
        logv = sb("logv", [TP, 2, TT])
        rstd = sb("rstd", [TP, 2, TT])
        shift_n = sb("shift_n", [TP, 2, TT])
        norm1 = sb("norm1", [TP, 2, TT, D])
        scaled = sb("scaled", [TP, 2, TT, D])
        sum_n = sb("sum_n", [TP, 2, TT, D])
        x1_n = sb("x1_n", [TP, 3, TT, D])
        resid_n = sb("resid_n", [TP, 3, TT, D])
        x1T_n = sb("x1T_n", [D, 3, TN])
        y_n = sb("y_n", [TP, 3, TT, D])
        n_at = [sem(f"n_at{s}") for s in range(3)]
        n_xin = [sem(f"n_xin{s}") for s in range(3)]
        n_ro = [sem(f"n_ro{s}") for s in range(3)]
        n_xTo = [sem(f"n_xTo{s}") for s in range(3)]
        n_yo = [sem(f"n_yo{s}") for s in range(3)]
        n_o, n_xo, n_xb, n_res, n_st, n_mv, n_log, n_rstd, n_sh, n_norm, n_scaled, n_sum, n_x1, n_rd, n_T, n_Tev, n_y, n_yev = [
            sem("n_" + s) for s in ("o", "xo", "xb", "res", "st", "mv", "log", "rstd", "sh", "norm", "scaled", "sum", "x1", "rd", "T", "Tev", "y", "yev")]
        STEPS = TILES + 3

        def norm_sync(sp):
            def body(i):
                if i.live():
                    wait(sp, n_o, i.n(-2))
                    sp.dma_start(at_in[:, i.slot(3), :], attT[:, bass.ds(i.n(0, TN), TN)]).then_inc(n_at[i.slot(3)], 16)
                    wait(sp, n_xb, i.n(-2))
                    sp.dma_start(xr_in[:, i.slot(3), :, :], rows_of(x, i)).then_inc(n_xin[i.slot(3)], 16)
                k = i.back(8)
                if k.live():
                    sp.wait_ge(n_rd, k.n(1))
                    apart(sp)
                    sp.dma_start(rows_of(resid_rows, k), resid_n[:, k.slot(3), :, :]).then_inc(n_ro[k.slot(3)], 16)
                    sp.wait_ge(n_Tev, k.n(1))
                    apart(sp)
                    sp.dma_start(xT_l[0][:, bass.ds(k.n(0, TN), TN)], x1T_n[:, k.slot(3), :]).then_inc(n_xTo[k.slot(3)], 16)
                    sp.wait_ge(n_yev, k.n(1))
                    apart(sp)
                    sp.dma_start(rows_of(y_table[0], k), y_n[:, k.slot(3), :, :]).then_inc(n_yo[k.slot(3)], 16)
            walk(sp, body, TILES, 8)
            for s in range(3):
                for o in (n_ro, n_xTo, n_yo):
                    sp.wait_ge(o[s], 16 * len(range(s, TILES, 3)))

        def norm_gpsimd(pool):
            def body(i):
                if i.live():
                    pool.wait_ge(n_xin[i.slot(3)], i.use(3, 1) * 16)
                    wait(pool, n_res, i.n(-2))
                    nc.gpsimd.tensor_tensor(xbout[:, i.slot(3), :, :], xr_in[:, i.slot(3), :, :],
                                            bout_bc[0:TP, :].unsqueeze(1).broadcast_to([TP, TT, D]), ALU.add).then_inc(n_xo, 1)
                    wait(pool, n_sum, i.n(1 - UNROLL))
                    nc.gpsimd.tensor_tensor(xbeta[:, i.slot(UNROLL), :, :], xr_in[:, i.slot(3), :, :],
                                            beta_bc[0:TP, :].unsqueeze(1).broadcast_to([TP, TT, D]), ALU.add).then_inc(n_xb, 1)
                k = i.back(6)
                if k.live():
                    pool.wait_ge(n_x1, k.n(1))
                    wait(pool, n_ro[k.slot(3)], k.use(3) * 16)
                    nc.gpsimd.tensor_tensor(resid_n[:, k.slot(3), :, :], x1_n[:, k.slot(3), :, :],
                                            dpb_bc[0:TP, :].unsqueeze(1).broadcast_to([TP, TT, D]), ALU.add).then_inc(n_rd, 1)
            walk(pool, body, TILES, 6)

        def norm_tensor(pe):
            def body(i):
                if i.live():
                    pe.wait_ge(n_at[i.slot(3)], i.use(3, 1) * 16)
                    wait(pe, n_res, i.n(-1))
                    for t in range(TT):
                        last = nc.tensor.matmul(bank[i.slot(2)][0:TP, t * D:(t + 1) * D], at_in[:, i.slot(3), t * TP:(t + 1) * TP],
                                                w_out_s[:], start=True, stop=True)
                    last.then_inc(n_o, 1)
                k = i.back(7)
                if k.live():
                    pe.wait_ge(n_Tev, k.n(1))
                    wait(pe, n_yev, k.n())
                    for t in range(TT):
                        last = nc.tensor.matmul(bank[3][0:TP, t * D:(t + 1) * D], x1T_n[:, k.slot(3), t * TP:(t + 1) * TP],
                                                psi_src_s[:, 0, :], start=True, stop=True)
                    last.then_inc(n_y, 1)
                j = i.back(6)
                if j.live():
                    pe.wait_ge(n_x1, j.n(1))
                    wait(pe, n_Tev, j.n())
                    apart(pe)
                    for t in range(TT):
                        last = nc.tensor.transpose(bank[2][:, t * TP:(t + 1) * TP], x1_n[:, j.slot(3), t, :], ident[0:TP, 0:TP])
                    last.then_inc(n_T, 1)
            walk(pe, body, TILES, 7)

        def norm_vector(dve):
            v = nc.vector
            v.memset(mean_var[:], 1.0).then_inc(n_mv, 1)
            dve.wait_ge(n_mv, 1)

            def body(i):
                first, second = i.back(1), i.back(4)
                if first.live():
                    dve.wait_ge(n_o, first.n(1))
                    dve.wait_ge(n_xo, first.n(1))
                    wait(dve, n_norm, first.n(-1))
                    v.tensor_tensor(flat(res_n[:, first.slot(2), :, :]), bank[first.slot(2)][0:TP, :], flat(xbout[:, first.slot(3), :, :]),
                                    ALU.add).then_inc(n_res, 1)
                p = At(i.turn, i.off - 2, STEPS)
                if p.live():
                    dve.wait_ge(n_rstd, p.n(1))
                    wait(dve, n_norm, p.n() if not p.fixed or p.n() < TILES else TILES)
                    wait(dve, n_x1, p.n(-3) if not p.fixed or p.n(-3) < TILES else TILES)
                    v.scalar_tensor_tensor(shift_n[:], mean_var[:, p.slot(2), :, :, 0], -1.0, rstd[:], ALU.mult, ALU.mult).then_inc(n_sh, 1)
                if second.live():
                    dve.wait_ge(n_scaled, second.n(1))
                    dve.wait_ge(n_xb, second.n(1))
                    wait(dve, n_x1, second.n(-1))
                    v.tensor_tensor(sum_n[:, second.slot(2), :, :], scaled[:, second.slot(2), :, :], xbeta[:, second.slot(UNROLL), :, :],
                                    ALU.add).then_inc(n_sum, 1)
                j = i.back(3)
                if j.live():
                    dve.wait_ge(n_norm, j.n(1))
                    wait(dve, n_sum, j.n(-1))
                    v.tensor_tensor(scaled[:, j.slot(2), :, :], norm1[:, j.slot(2), :, :],
                                    gamma_bc[0:TP, :].unsqueeze(1).broadcast_to([TP, TT, D]), ALU.mult).then_inc(n_scaled, 1)
                if first.live():
                    dve.wait_ge(n_res, first.n(1))
                    for t in range(TT):
                        last = v.bn_stats(stats[:, 0, t, :], res_n[:, first.slot(2), t, :])
                if second.live():
                    dve.wait_ge(n_sum, second.n(1))
                    for t in range(TT):
                        last = v.bn_stats(stats[:, 1, t, :], sum_n[:, second.slot(2), t, :])
                if first.live() or second.live():
                    last.then_inc(n_st, 1)
                if first.live() or second.live():
                    dve.wait_ge(n_st, i.n())
                    apart(dve)
                    for which, tile in ((0, first), (1, second)):
                        if tile.live():
                            for t in range(TT):
                                last = v.bn_aggr(mean_var[:, (i.off - 1) % 2, which, t, :], stats[:, which, t, :])
                    last.then_inc(n_mv, 1)
            walk(dve, body, TILES, 5)

        def norm_scalar(act):
            def body(i):
                p = At(i.turn, i.off - 2, STEPS)
                if p.live():
                    act.wait_ge(n_mv, p.n(2))
                    wait(act, n_sh, p.n())
                    nc.scalar.activation(logv[:], mean_var[:, p.slot(2), :, :, 1], ACT.Ln, bias=eps_col[0:TP, 0:1]).then_inc(n_log, 1)
                k, y = i.back(6), i.back(7)
                if y.live():
                    act.wait_ge(n_y, y.n(1))
                    wait(act, n_yo[y.slot(3)], y.use(3) * 16)
                    nc.scalar.copy(flat(y_n[:, y.slot(3), :, :]), bank[3][0:TP, :]).then_inc(n_yev, 1)
                if p.live():
                    act.wait_ge(n_log, p.n(1))
                    nc.scalar.activation(rstd[:], logv[:], ACT.Exp, scale=-0.5).then_inc(n_rstd, 1)
                if k.live():
                    act.wait_ge(n_T, k.n(1))
                    wait(act, n_xTo[k.slot(3)], k.use(3) * 16)
                    nc.scalar.copy(x1T_n[:, k.slot(3), :], bank[2][:, 0:TN]).then_inc(n_Tev, 1)
                first, second = i.back(2), i.back(5)
                if p.live():
                    act.wait_ge(n_sh, p.n(1))
                if second.live():
                    wait(act, n_rd, second.n(-2))
                    wait(act, n_T, second.n(-2))
                    for t in range(TT):
                        last = nc.scalar.activation(x1_n[:, second.slot(3), t, :], sum_n[:, second.slot(2), t, :], ACT.Identity,
                                                    bias=shift_n[:, 1, t:t + 1], scale=rstd[:, 1, t:t + 1])
                    last.then_inc(n_x1, 1)
                if first.live():
                    wait(act, n_scaled, first.n(-1))
                    for t in range(TT):
                        last = nc.scalar.activation(norm1[:, first.slot(2), t, :], res_n[:, first.slot(2), t, :], ACT.Identity,
                                                    bias=shift_n[:, 0, t:t + 1], scale=rstd[:, 0, t:t + 1])
                    last.then_inc(n_norm, 1)
            walk(act, body, TILES, 7)

        give_back()
        z_b = hd_b
        m_b = leaky_b
        agg_b = sb("agg_b", [D, 2, BN])
        relu_b = sb("relu_b", [D, BN])
        xnew_b = sb("xnew_b", [D, UNROLL, BN])
        yrow_b = sb("yrow_b", [CP, UNROLL, CT, D])
        x1_b = sb("x1_b", [CP, 3, CT, D])
        fstats = sb("fstats", [CP, CT, 6])
        fmv = sb("fmv", [CP, 2, CT, 2])
        flog = sb("flog", [CP, CT])
        frstd = sb("frstd", [CP, 2, CT])
        fshift = sb("fshift", [CP, 2, CT])
        fsum = sb("fsum", [CP, 3, CT, D])
        def block_rows(table, i):
            return table[bass.ds(i.n(0, BN), BN), :].rearrange("(c p) d -> p c d", p=CP)

        def layer_sync(sp, l):
            base = l * BATCHES
            last_layer = l == LAYERS - 1
            lag = 8 if last_layer else 6

            def body(i):
                if i.live():
                    if not i.fixed or i.n() >= UNROLL:
                        sp.wait_ge(g_xnew, i.n(base + 1 - UNROLL))
                    sp.dma_start(xt_b[:, i.slot(UNROLL), :], xT_l[l][:, bass.ds(i.n(0, BN), BN)]).then_inc(x_in[i.slot(UNROLL)], 16)
                    wait(sp, g_slot1h, i.n(base - 2))
                    sp.dma_start(dl_b[:, i.slot(3), :].unsqueeze(1),
                                 dloc_d[bass.ds(i.n(0, K), K), :].rearrange("k s -> (k s)").partition_broadcast(NB)
                                 ).then_inc(dl_in[i.slot(3)], 16)
                j = i.back(3)
                if last_layer and j.live():
                    wait(sp, f_sum, j.n(-2))
                    sp.dma_start(x1_b[:, j.slot(3), :, :], block_rows(resid_rows, j)).then_inc(g_x1[j.slot(3)], 16)
                k = i.back(lag)
                if k.live():
                    if not last_layer:
                        sp.wait_ge(g_xnew, k.n(base + 1))
                        sp.dma_start(xT_l[l + 1][:, bass.ds(k.n(0, BN), BN)], xnew_b[:, k.slot(UNROLL), :]).then_inc(cols_out[k.slot(UNROLL)], 16)
                    sp.wait_ge(g_yev, k.n(base + 1))
                    sp.dma_start(block_rows(out if last_layer else y_table[l + 1], k), yrow_b[:, k.slot(UNROLL), :, :]
                                 ).then_inc(g_yo[k.slot(UNROLL)], 16)
            walk(sp, body, BATCHES, lag)
            for s in range(UNROLL):
                sp.wait_ge(g_yo[s], 16 * uses(UNROLL, l + 1)[s])
                sp.wait_ge(cols_out[s], 16 * uses(UNROLL, min(l + 2, LAYERS))[s])

        def layer_gpsimd(pool, l):
            def body(i):
                if i.live():
                    gather(pool, i, y_table[l], g_idx, rows_in, g_pre, l * BATCHES)
            walk(pool, body, BATCHES, 0)

        def layer_tensor(pe, l):
            base, ins, turns = l * BATCHES, uses(UNROLL, l + 1), uses(UNROLL, l)
            last_layer = l == LAYERS - 1
            last_w = dp_s[:] if last_layer else psi_src_s[:, l + 1, :]

            def body(i):
                j, k, q, y = i.back(1), i.back(2), i.back(3), i.back(4)
                if i.live():
                    pe.wait_ge(x_in[i.slot(UNROLL)], (i.use(UNROLL, 1) + ins[i.slot(UNROLL)]) * 16)
                    wait(pe, g_zev, i.n(base))
                    for b in range(K):
                        last = nc.tensor.matmul(wide[0][0:NB, b * D:(b + 1) * D], xt_b[:, i.slot(UNROLL), b * NB:(b + 1) * NB],
                                                psi_dst_s[:, l, :], start=True, stop=True)
                    last.then_inc(g_z, 1)
                if j.live():
                    pe.wait_ge(g_zev, j.n(base + 1))
                    pe.wait_ge(g_slot1h, j.n(base + 1))
                    wait(pe, g_pre, j.n(base))
                    for b in range(K):
                        last = nc.tensor.matmul(wide[1][:, b * D:(b + 1) * D], to_slot[:, j.slot(2), b * SLOTS:(b + 1) * SLOTS],
                                                z_b[:, j.slot(2), b * D:(b + 1) * D], start=True, stop=True)
                    last.then_inc(g_u, 1)
                if k.live():
                    pe.wait_ge(g_m, k.n(base + 1))
                    pe.wait_ge(g_node1h, k.n(base + 1))
                    wait(pe, g_aggev, k.n(base))
                    for b in range(K):
                        last = nc.tensor.matmul(bank[0][:, b * NB:(b + 1) * NB], m_b[:, k.slot(2), b * D:(b + 1) * D],
                                                to_node[:, k.slot(2), b, :], start=True, stop=True)
                    last.then_inc(g_agg, 1)
                if q.live():
                    pe.wait_ge(g_aggev, q.n(base + 1))
                    wait(pe, g_relu, q.n(base))
                    nc.tensor.matmul(bank[1][:, 0:BN], phi_x_s[:, l, :], xt_b[:, q.slot(UNROLL), :], start=True, stop=False)
                    nc.tensor.matmul(bank[1][:, 0:BN], phi_agg_s[:, l, :], agg_b[:, q.slot(2), :], start=False, stop=True).then_inc(g_q, 1)
                if y.live():
                    pe.wait_ge(g_xnew, y.n(base + 1))
                    if last_layer:
                        wait(pe, f_sum, y.n(-1))
                    wait(pe, g_yev, y.n(base - 1) if not last_layer else base)
                    for c in range(CT):
                        last = nc.tensor.matmul(bank[2 + y.slot(2)][0:CP, c * D:(c + 1) * D], xnew_b[:, y.slot(UNROLL), c * CP:(c + 1) * CP],
                                                last_w, start=True, stop=True)
                    last.then_inc(g_y, 1)
            walk(pe, body, BATCHES, 4)

        def layer_scalar(act, l):
            base, ins, turns = l * BATCHES, uses(UNROLL, l + 1), uses(UNROLL, l)
            last_layer = l == LAYERS - 1

            def body(i):
                j, k, q, y = i.back(1), i.back(2), i.back(3), i.back(4)
                f, g = i.back(6), i.back(7)
                if last_layer and f.live():
                    act.wait_ge(f_mv, f.n(1))
                    wait(act, f_rstd, f.n())
                    nc.scalar.activation(flog[:].unsqueeze(2), fmv[:, f.slot(2), :, 1:2], ACT.Ln, bias=eps_col[0:CP, 0:1]).then_inc(f_log, 1)
                    act.wait_ge(f_log, f.n(1))
                    nc.scalar.activation(frstd[:, f.slot(2), :], flog[:], ACT.Exp, scale=-0.5).then_inc(f_rstd, 1)
                if last_layer and g.live():
                    act.wait_ge(f_sh, g.n(1))
                    wait(act, g_yo[g.slot(UNROLL)], (g.use(UNROLL) + turns[g.slot(UNROLL)]) * 16)
                    for c in range(CT):
                        last = nc.scalar.activation(yrow_b[:, g.slot(UNROLL), c, :], fsum[:, g.slot(3), c, :], ACT.Identity,
                                                    bias=fshift[:, g.slot(2), c:c + 1], scale=frstd[:, g.slot(2), c:c + 1])
                    last.then_inc(g_yev, 1)
                if k.live():
                    act.wait_ge(g_agg, k.n(base + 1))
                    wait(act, g_q, k.n(base - 1))
                    nc.scalar.copy(agg_b[:, k.slot(2), :], bank[0][:, 0:BN]).then_inc(g_aggev, 1)
                if q.live():
                    act.wait_ge(g_q, q.n(base + 1))
                    wait(act, g_xnew, q.n(base))
                    nc.scalar.activation(relu_b[:], bank[1][:, 0:BN], ACT.Relu, bias=phi_b_col[:, l:l + 1]).then_inc(g_relu, 1)
                if j.live():
                    act.wait_ge(g_pre, j.n(base + 1))
                    wait(act, g_agg, j.n(base - 1))
                    nc.scalar.activation(m_b[:, j.slot(2), :], pre_b[:, j.slot(2), :], ACT.Relu).then_inc(g_m, 1)
                if y.live() and not last_layer:
                    act.wait_ge(g_y, y.n(base + 1))
                    wait(act, g_yo[y.slot(UNROLL)], (y.use(UNROLL) + turns[y.slot(UNROLL)]) * 16)
                    nc.scalar.copy(yrow_b[:, y.slot(UNROLL), :, :].rearrange("p c d -> p (c d)"), bank[2 + y.slot(2)][0:CP, :]).then_inc(g_yev, 1)
            walk(act, body, BATCHES, 7 if last_layer else 4)

        def layer_vector(dve, l):
            base, ins, turns = l * BATCHES, uses(UNROLL, l + 1), uses(UNROLL, l)
            last_layer = l == LAYERS - 1
            v = nc.vector
            first_indices(g_idx)

            def body(i):
                j, q = i.back(1), i.back(3)
                f, g = i.back(5), i.back(6)
                if last_layer and f.live():
                    dve.wait_ge(g_y, f.n(base + 1))
                    dve.wait_ge(g_x1[f.slot(3)], f.use(3, 1) * 16)
                    wait(dve, g_yev, f.n(base - 2))
                    v.tensor_tensor(fsum[:, f.slot(3), :, :], bank[2 + f.slot(2)][0:CP, :].rearrange("p (c d) -> p c d", d=D),
                                    x1_b[:, f.slot(3), :, :], ALU.add).then_inc(f_sum, 1)
                if i.live():
                    slot_one_hot(dve, i, dl_in, g_u, g_slot1h, base, uses(3, l + 1))
                    dve.wait_ge(g_z, i.n(base + 1))
                    v.tensor_tensor(z_b[:, i.slot(2), :].rearrange("p (k d) -> p k d", k=K), wide[0][0:NB, 0:BS].rearrange("p (k d) -> p k d", k=K),
                                    psi_b_bc[0:NB, l, :].unsqueeze(1).broadcast_to([NB, K, D]), ALU.add).then_inc(g_zev, 1)
                if last_layer and f.live():
                    dve.wait_ge(f_sum, f.n(1))
                    for c in range(CT):
                        last = v.bn_stats(fstats[:, c, :], fsum[:, f.slot(3), c, :])
                    last.then_inc(f_st, 1)
                if j.live():
                    wait(dve, g_agg, j.n(base - 1))
                    for b in range(K):
                        last = v.tensor_scalar(to_node[:, j.slot(2), b, :], iota_row[:, 0:NB], dloc_c[:, bass.ds(j.n(0, K) + b, 1)],
                                               invdeg_c[:, bass.ds(j.n(0, K) + b, 1)], ALU.is_equal, ALU.mult)
                    last.then_inc(g_node1h, 1)
                    dve.wait_ge(g_u, j.n(base + 1))
                    dve.wait_ge(rows_in[j.slot(UNROLL)], (j.use(UNROLL, 1) + ins[j.slot(UNROLL)]) * 16 * K)
                    wait(dve, g_m, j.n(base - 1))
                    v.tensor_tensor(pre_b[:, j.slot(2), :], wide[1][:, 0:K * D], rows_b[:, j.slot(UNROLL), :, :].rearrange("p k d -> p (k d)"),
                                    ALU.add).then_inc(g_pre, 1)
                    next_indices(j, g_idx)
                if last_layer and f.live():
                    dve.wait_ge(f_st, f.n(1))
                    apart(dve)
                    for c in range(CT):
                        last = v.bn_aggr(fmv[:, f.slot(2), c, :], fstats[:, c, :])
                    last.then_inc(f_mv, 1)
                if last_layer and g.live():
                    dve.wait_ge(f_rstd, g.n(1))
                    v.scalar_tensor_tensor(fshift[:, g.slot(2), :].unsqueeze(2), fmv[:, g.slot(2), :, 0:1], -1.0, frstd[:, g.slot(2), :].unsqueeze(2),
                                           ALU.mult, ALU.mult).then_inc(f_sh, 1)
                if q.live():
                    dve.wait_ge(g_relu, q.n(base + 1))
                    if not last_layer:
                        wait(dve, cols_out[q.slot(UNROLL)], (q.use(UNROLL) + ins[q.slot(UNROLL)]) * 16)
                    wait(dve, g_y, q.n(base + 1 - UNROLL) if not q.fixed or q.n() >= UNROLL else base)
                    v.tensor_tensor(xnew_b[:, q.slot(UNROLL), :], relu_b[:], xt_b[:, q.slot(UNROLL), :], ALU.add).then_inc(g_xnew, 1)
            walk(dve, body, BATCHES, 6 if last_layer else 3, reach=UNROLL - 1)

        with nc.Block() as block:
            @block.sync
            def _(sp):
                prep_sync(sp)
                table_sync(sp)
                tables_sync(sp)
                sp.sem_inc(phase_done, 1)

                def slow():
                    zero_sync(sp)
                    general(sp, node_sync, edge_sync, 0, len(ATTEND))
                by_path(sp, lambda: att_sync(sp), slow)
                sp.sem_inc(phase_done, 1)
                norm_sync(sp)
                sp.sem_inc(phase_done, 1)

                def fast_layers():
                    for l in range(LAYERS):
                        layer_sync(sp, l)
                        sp.sem_inc(phase_done, 1)
                by_path(sp, fast_layers, lambda: general(sp, node_sync, edge_sync, len(ATTEND), len(PLAN)))

            @block.gpsimd
            def _(pool):
                prep_gpsimd(pool)
                begin(pool, 1)
                by_path(pool, lambda: att_gpsimd(pool), lambda: general(pool, None, edge_gpsimd, 0, len(ATTEND)))
                begin(pool, 2)
                norm_gpsimd(pool)

                def fast_layers():
                    for l in range(LAYERS):
                        begin(pool, 3 + l)
                        layer_gpsimd(pool, l)
                by_path(pool, fast_layers, lambda: general(pool, None, edge_gpsimd, len(ATTEND), len(PLAN)))

            @block.tensor
            def _(pe):
                table_tensor(pe)
                columns_tensor(pe)
                begin(pe, 1)
                by_path(pe, lambda: att_tensor(pe), lambda: general(pe, node_tensor, edge_tensor, 0, len(ATTEND)))
                begin(pe, 2)
                norm_tensor(pe)

                def fast_layers():
                    for l in range(LAYERS):
                        begin(pe, 3 + l)
                        layer_tensor(pe, l)
                by_path(pe, fast_layers, lambda: general(pe, node_tensor, edge_tensor, len(ATTEND), len(PLAN)))

            @block.scalar
            def _(act):
                nc.scalar.preload_act_table_set("natural_log_exp_and_others")
                table_scalar(act)
                begin(act, 1)
                by_path(act, lambda: att_scalar(act), lambda: general(act, node_scalar, edge_scalar, 0, len(ATTEND)))
                begin(act, 2)
                norm_scalar(act)

                def fast_layers():
                    for l in range(LAYERS):
                        begin(act, 3 + l)
                        layer_scalar(act, l)
                by_path(act, fast_layers, lambda: general(act, node_scalar, edge_scalar, len(ATTEND), len(PLAN)))

            @block.vector
            def _(dve):
                prep_vector(dve)
                begin(dve, 1)

                def slow():
                    zero_vector(dve)
                    general(dve, node_vector, edge_vector, 0, len(ATTEND))
                by_path(dve, lambda: att_vector(dve), slow)
                begin(dve, 2)
                norm_vector(dve)

                def fast_layers():
                    for l in range(LAYERS):
                        begin(dve, 3 + l)
                        layer_vector(dve, l)
                by_path(dve, fast_layers, lambda: general(dve, node_vector, edge_vector, len(ATTEND), len(PLAN)))


def kernel(**inputs):
    import numpy as np
    import concourse.bacc as bacc
    from concourse.bass_utils import run_bass_kernel_spmd

    a = {name: np.asarray(value) for name, value in inputs.items()}
    src = np.zeros([EROWS * SLOTS], np.int32)
    dst = np.full([EROWS * SLOTS], 1 << 20, np.int32)
    src[:E] = a["src"]
    dst[:E] = a["dst"]
    psi, phi = a["L1_gnn_psi_w"], a["L1_gnn_phi_w"]
    arrays = {
        "xT": a["x"].T, "x": a["x"],
        "src_dst": np.stack([src.reshape(EROWS, SLOTS), dst.reshape(EROWS, SLOTS)], axis=1).reshape(EROWS, 2 * SLOTS),
        "dst_cols": a["dst"].reshape(GP, EC), "src_flat": a["src"].reshape(E, 1),
        "dst_pad": np.concatenate([np.full(1, -1, np.int32), a["dst"], np.full(1, -1, np.int32)]).reshape(E + 2, 1),
        "w_src": a["L0_gnn_W_src"], "w_dst": a["L0_gnn_W_dst"], "attn": a["L0_gnn_attn"].reshape(1, D),
        "w_out": a["L0_gnn_W_out"], "b_out": a["L0_gnn_b_out"].reshape(1, D),
        "gamma": a["L0_gnn_gamma"].reshape(1, D), "beta": a["L0_gnn_beta"].reshape(1, D),
        "psi_dst": psi[:, :D, :], "psi_src": psi[:, D:, :], "psi_b": a["L1_gnn_psi_b"],
        "phi_x": phi[:, :D, :], "phi_agg": phi[:, D:, :], "phi_b": a["L1_gnn_phi_b"].T,
        "dp_w": a["L1_gnn_dp_w"], "dp_b": a["L1_gnn_dp_b"].reshape(1, D),
    }
    nc = bacc.Bacc("TRN2", target_bir_lowering=False, num_devices=1)
    given, args = {}, []
    for name, value in arrays.items():
        value = np.ascontiguousarray(value)
        given["in_" + name] = value
        args.append(nc.dram_tensor("in_" + name, value.shape, mybir.dt.from_np(value.dtype), kind="ExternalInput").ap())
    args.append(nc.dram_tensor("out_x", [N, D], FP32, kind="ExternalOutput").ap())
    gnn_kernel(nc, *args)
    return run_bass_kernel_spmd(nc, [given], core_ids=[0]).results[0]["out_x"]
```
